# Optimizing a Trainium2 kernel written in Bass

```python
import numpy as np
import jax
import jax.numpy as jnp

def _softmax(x, axis=-1):
    return jax.nn.softmax(x, axis=axis)

def _gelu(x):
    return jax.nn.gelu(x, approximate=True)

def _silu(x):
    return jax.nn.silu(x)

def _sigmoid(x):
    return jax.nn.sigmoid(x)

def _layernorm(x, axis=-1, eps=1e-05):
    m = jnp.mean(x, axis=axis, keepdims=True)
    v = jnp.var(x, axis=axis, keepdims=True)
    return (x - m) / jnp.sqrt(v + eps)

def _scatter_add(tgt, idx, src, axis=0):
    return tgt.at[idx].add(src)

def _segment_sum(src, seg, n):
    return jax.ops.segment_sum(src, seg, n)
kernel_name = 'mk_adj_ffn_d2_adj_r2_7a8c9c'

def setup_inputs(seed: int=0):
    np.random.seed(seed)
    _w = jnp.asarray

    def _rec_inputs():
        import jax
        import jax.numpy as jnp
        _gk = jax.random.key(seed)
        x = -0.000929 + 1 * jax.random.normal(jax.random.fold_in(_gk, 1), (2048, 128), jnp.float32)
        _a = jax.random.bernoulli(jax.random.fold_in(_gk, 2), 0.0078125, (2048, 2048))
        _a = jnp.logical_or(_a, jnp.swapaxes(_a, -1, -2))
        _a = jnp.logical_or(_a, jnp.eye(2048, dtype=bool))
        adj = _a.astype(jnp.int32)
        return (x, adj)
    x, adj = _rec_inputs()

    def _L0_gnn_setup():
        import jax, jax.numpy as jnp
        import numpy as np
        N = 2048
        IN_DIM = 128
        OUT_DIM = 128
        H = 4
        D = OUT_DIM // H
        ALPHA = 0.2
        NEG_INF = -9000000000000000.0
        key = jax.random.key(seed)
        k1, k2, k3, k4, k5 = jax.random.split(key, 5)
        h = jax.random.normal(k1, (N, IN_DIM), dtype=jnp.float32)
        adj = jax.random.randint(k2, (N, N), 0, 2, dtype=jnp.int32)
        lim_w = 1.414 * np.sqrt(6.0 / (IN_DIM + H * D))
        W = jax.random.uniform(k3, (H * D, IN_DIM), dtype=jnp.float32, minval=-lim_w, maxval=lim_w)
        b = jnp.zeros((H * D,), dtype=jnp.float32)
        lim_a = 1.414 * np.sqrt(6.0 / (H + 2 * D))
        a = jax.random.uniform(k4, (H, 2 * D), dtype=jnp.float32, minval=-lim_a, maxval=lim_a)
        return {'h': h, 'adj': adj, 'W': W, 'b': b, 'a': a}
    _L0_gnn_all = _L0_gnn_setup()
    _L0_gnn_in = {k: v for k, v in _L0_gnn_all.items() if k in ('W', 'b', 'a')}
    del _L0_gnn_all

    def _L0_ffn_setup():
        import jax, jax.numpy as jnp
        import numpy as np
        B, S, D, H, E, K = (8, 4096, 128, 512, 8, 2)
        key = jax.random.key(seed)
        ks = jax.random.split(key, 7)
        s_in = 1.0 / np.sqrt(D)
        s_hid = 1.0 / np.sqrt(H)
        return {'x': jax.random.normal(ks[0], (B, S, D), dtype=jnp.float32), 'Wg': jax.random.uniform(ks[1], (E, D), jnp.float32, -s_in, s_in), 'bg': jax.random.uniform(ks[2], (E,), jnp.float32, -s_in, s_in), 'W1': jax.random.uniform(ks[3], (E, H, D), jnp.float32, -s_in, s_in), 'b1': jax.random.uniform(ks[4], (E, H), jnp.float32, -s_in, s_in), 'W2': jax.random.uniform(ks[5], (E, D, H), jnp.float32, -s_hid, s_hid), 'b2': jax.random.uniform(ks[6], (E, D), jnp.float32, -s_hid, s_hid)}
    _L0_ffn_all = _L0_ffn_setup()
    _L0_ffn_in = {k: v for k, v in _L0_ffn_all.items() if k in ('Wg', 'bg', 'W1', 'b1', 'W2', 'b2')}
    del _L0_ffn_all

    def _L1_gnn_setup():
        import jax, jax.numpy as jnp
        import numpy as np
        N_HEADS = 4
        key = jax.random.key(seed)
        k1, k2, k3, k4 = jax.random.split(key, 4)
        N, IN, OUT = (2048, 128, 128)
        x = jax.random.normal(k1, (N, IN), dtype=jnp.float32)
        adj = jax.random.randint(k2, (N, N), 0, 2, dtype=jnp.int32)
        W = jax.random.normal(k3, (OUT, IN), dtype=jnp.float32) * 0.05
        d_k = OUT // N_HEADS
        a = jax.random.normal(k4, (2 * d_k, 1), dtype=jnp.float32) * 0.05
        return {'x': x, 'adj': adj, 'W': W, 'a': a}
    _L1_gnn_all = _L1_gnn_setup()
    _L1_gnn_in = {k: v for k, v in _L1_gnn_all.items() if k in ('W', 'a')}
    del _L1_gnn_all

    def _L1_ffn_setup():
        import jax, jax.numpy as jnp
        import numpy as np
        B, T, IN_DIM = (64, 128, 128)
        HID, OUT_DIM = (256, 128)
        N_LAYERS, N_EXPERTS, N_SHARED = (2, 16, 1)
        key = jax.random.key(seed)
        ks = jax.random.split(key, 10)
        s = 0.02
        x = jax.random.normal(ks[0], (B, T, IN_DIM), dtype=jnp.float32)
        route_id = jax.random.randint(ks[1], (B,), 0, N_EXPERTS)
        Wi = jax.random.normal(ks[2], (HID, IN_DIM), dtype=jnp.float32) * s
        bi = jnp.zeros((HID,), dtype=jnp.float32)
        Wr = jax.random.normal(ks[3], (N_LAYERS, N_EXPERTS, HID, HID), dtype=jnp.float32) * s
        br = jax.random.normal(ks[4], (N_LAYERS, N_EXPERTS, HID), dtype=jnp.float32) * s
        Ws = jax.random.normal(ks[5], (N_LAYERS, N_SHARED, HID, HID), dtype=jnp.float32) * s
        bs = jax.random.normal(ks[6], (N_LAYERS, N_SHARED, HID), dtype=jnp.float32) * s
        Wo = jax.random.normal(ks[7], (OUT_DIM, HID), dtype=jnp.float32) * s
        bo = jnp.zeros((OUT_DIM,), dtype=jnp.float32)
        return {'x': x, 'route_id': route_id, 'Wi': Wi, 'bi': bi, 'Wr': Wr, 'br': br, 'Ws': Ws, 'bs': bs, 'Wo': Wo, 'bo': bo}
    _L1_ffn_all = _L1_ffn_setup()
    _L1_ffn_in = {k: v for k, v in _L1_ffn_all.items() if k in ('route_id', 'Wi', 'bi', 'Wr', 'br', 'Ws', 'bs', 'Wo', 'bo')}
    del _L1_ffn_all
    return {'x': x, 'adj': adj, 'L0_gnn_W': _L0_gnn_in['W'], 'L0_gnn_b': _L0_gnn_in['b'], 'L0_gnn_a': _L0_gnn_in['a'], 'L0_ffn_Wg': _L0_ffn_in['Wg'], 'L0_ffn_bg': _L0_ffn_in['bg'], 'L0_ffn_W1': _L0_ffn_in['W1'], 'L0_ffn_b1': _L0_ffn_in['b1'], 'L0_ffn_W2': _L0_ffn_in['W2'], 'L0_ffn_b2': _L0_ffn_in['b2'], 'L1_gnn_W': _L1_gnn_in['W'], 'L1_gnn_a': _L1_gnn_in['a'], 'L1_ffn_route_id': _L1_ffn_in['route_id'], 'L1_ffn_Wi': _L1_ffn_in['Wi'], 'L1_ffn_bi': _L1_ffn_in['bi'], 'L1_ffn_Wr': _L1_ffn_in['Wr'], 'L1_ffn_br': _L1_ffn_in['br'], 'L1_ffn_Ws': _L1_ffn_in['Ws'], 'L1_ffn_bs': _L1_ffn_in['bs'], 'L1_ffn_Wo': _L1_ffn_in['Wo'], 'L1_ffn_bo': _L1_ffn_in['bo']}

def reference(x, adj, L0_gnn_W, L0_gnn_b, L0_gnn_a, L0_ffn_Wg, L0_ffn_bg, L0_ffn_W1, L0_ffn_b1, L0_ffn_W2, L0_ffn_b2, L1_gnn_W, L1_gnn_a, L1_ffn_route_id, L1_ffn_Wi, L1_ffn_bi, L1_ffn_Wr, L1_ffn_br, L1_ffn_Ws, L1_ffn_bs, L1_ffn_Wo, L1_ffn_bo):
    import jax
    import jax.numpy as jnp

    def _L0_gnn_ref(h, adj, W, b, a):
        import jax, jax.numpy as jnp
        import numpy as np
        N = 2048
        IN_DIM = 128
        OUT_DIM = 128
        H = 4
        D = OUT_DIM // H
        ALPHA = 0.2
        NEG_INF = -9000000000000000.0
        Wh = (h @ W.T + b).reshape(N, H, D)
        src = jnp.einsum('nhd,hd->nh', Wh, a[:, :D])
        dst = jnp.einsum('nhd,hd->nh', Wh, a[:, D:])
        e = src[:, None, :] + dst[None, :, :]
        e = jax.nn.leaky_relu(e, negative_slope=ALPHA)
        att = jnp.where(adj[:, :, None] == 1, e, NEG_INF)
        att = jax.nn.softmax(att, axis=1)
        h_prime = jnp.einsum('ijh,jhd->ihd', att, Wh)
        return h_prime.reshape(N, H * D)

    def _L0_ffn_ref(x, Wg, bg, W1, b1, W2, b2):
        import jax, jax.numpy as jnp
        import numpy as np
        B, S, D, H, E, K = (8, 4096, 128, 512, 8, 2)
        gate_scores = jnp.einsum('bsd,ed->bse', x, Wg) + bg
        topk_scores, topk_idx = jax.lax.top_k(gate_scores, K)
        topk_probs = jax.nn.softmax(topk_scores, axis=-1)
        combine = jnp.sum(topk_probs[..., None] * jax.nn.one_hot(topk_idx, E, dtype=x.dtype), axis=-2)
        out = jnp.zeros_like(x)
        for e in range(E):
            h = jax.nn.relu(jnp.einsum('bsd,hd->bsh', x, W1[e]) + b1[e])
            y = jnp.einsum('bsh,dh->bsd', h, W2[e]) + b2[e]
            out = out + combine[..., e:e + 1] * y
        return out

    def _L1_gnn_ref(x, adj, W, a):
        import jax, jax.numpy as jnp
        import numpy as np
        N_HEADS = 4
        H = N_HEADS
        N = x.shape[0]
        Wh = x @ W.T
        d_k = Wh.shape[-1] // H
        Whh = Wh.reshape(N, H, d_k)
        a1 = a[:d_k, 0]
        a2 = a[d_k:, 0]
        s1 = jnp.einsum('nhd,d->nh', Whh, a1)
        s2 = jnp.einsum('nhd,d->nh', Whh, a2)
        z = s1[:, None, :] + s2[None, :, :]
        e = jnp.where(z > 0, z, 0.2 * z).mean(-1)
        attn = jnp.where(adj > 0, e, jnp.float32(-9000000000000000.0))
        attn = jax.nn.softmax(attn, axis=1)
        out = jnp.einsum('ij,jhd->ihd', attn, Whh)
        return out.reshape(N, H * d_k)

    def _L1_ffn_ref(x, route_id, Wi, bi, Wr, br, Ws, bs, Wo, bo):
        import jax, jax.numpy as jnp
        import numpy as np
        B, T, IN_DIM = (64, 128, 128)
        HID, OUT_DIM = (256, 128)
        N_LAYERS, N_EXPERTS, N_SHARED = (2, 16, 1)
        flat = x.reshape(-1, x.shape[-1])
        n_tok = flat.shape[0]
        route = jnp.repeat(route_id, n_tok // route_id.shape[0])
        h = jax.nn.relu(flat @ Wi.T + bi)
        n_layers, n_experts = (Wr.shape[0], Wr.shape[1])
        for l in range(n_layers):
            shared = (jnp.einsum('nd,shd->snh', h, Ws[l]) + bs[l][:, None, :]).mean(axis=0)
            routed = jnp.zeros_like(h)
            for e in range(n_experts):
                ye = h @ Wr[l, e].T + br[l, e]
                routed = routed + jnp.where((route == e)[:, None], ye, 0.0)
            h = jax.nn.relu(shared + routed + h)
        out = h @ Wo.T + bo
        return out.reshape(*x.shape[:-1], out.shape[-1])
    x = x + _L0_gnn_ref(_layernorm(x, axis=-1), adj, L0_gnn_W, L0_gnn_b, L0_gnn_a)
    x = x + _L0_ffn_ref(_layernorm(x, axis=-1)[None], L0_ffn_Wg, L0_ffn_bg, L0_ffn_W1, L0_ffn_b1, L0_ffn_W2, L0_ffn_b2)[0]
    x = x + _L1_gnn_ref(_layernorm(x, axis=-1), adj, L1_gnn_W, L1_gnn_a)
    x = x + _L1_ffn_ref(_layernorm(x, axis=-1)[None], L1_ffn_route_id, L1_ffn_Wi, L1_ffn_bi, L1_ffn_Wr, L1_ffn_br, L1_ffn_Ws, L1_ffn_bs, L1_ffn_Wo, L1_ffn_bo)[0]
    return x

_drawn_inputs = setup_inputs


def setup_inputs(seed=0):
    import zlib

    import numpy as np

    out = dict(_drawn_inputs(seed))
    spreads = {'L0_gnn_b': (0.0, 0.1), 'L1_ffn_bi': (0.0, 0.467), 'L1_ffn_bo': (0.0, 0.1)}
    factors = {'L0_ffn_b1': 4.601,
     'L0_ffn_b2': 3.526,
     'L1_gnn_a': 8.0,
     'L1_ffn_Wr': 3.401,
     'L1_ffn_br': 8.0,
     'L1_ffn_Ws': 3.438,
     'L1_ffn_bs': 8.0}
    for name, (base, spread) in spreads.items():
        noise = np.random.default_rng([zlib.crc32(name.encode()), seed]).standard_normal(out[name].shape)
        drawn = base * np.exp(spread * noise) if base else spread * noise
        out[name] = jnp.asarray(drawn.astype(out[name].dtype))
    for name, factor in factors.items():
        out[name] = (out[name] * factor).astype(out[name].dtype)
    return out
```

```python
from contextlib import ExitStack

import numpy as np

import concourse.bass as bass
from concourse import mybir

ALU = mybir.AluOpType
ACT = mybir.ActivationFunctionType
F32 = mybir.dt.float32
BF16 = mybir.dt.bfloat16
I32 = mybir.dt.int32
AX_X = mybir.AxisListType.X
RMAX = bass.bass_isa.ReduceOp.max

P = 128
N = 2048
T = N // P
CT = 4
C = T // CT
CW = CT * P
H = 4
DH = P // H
V1 = DH + 1
PARTS = 3
VW = PARTS * V1
QT = 4
Q = T // QT
E0 = 8
HC = 4
E1 = 16
HID = 256
KC = HID // P
L = 2
GRP = 32
GT = P // GRP
EPS = 1e-5
SLOPE = 0.2
SHIFT = 60.0
NEG = -3.0e38
XC = P + 2 * H


class Count:

    def __init__(self):
        self.n, self.off, self.bank = {}, {}, {}

    def event(self, name, by=1):
        self.n[name] = self.n.get(name, 0) + by
        return self.at(name)

    def at(self, name):
        return self.off.get(name, 0) + self.n.get(name, 0)

    def fill(self, b, name):
        self.event(name)
        self.bank[b] = (name, self.n[name])

    def freed(self, b):
        name, n = self.bank[b]
        return name, self.off.get(name, 0) + n

    def enter(self, i, first, per):
        self.at_entry = dict(self.n), dict(self.off), dict(self.bank)
        for name, by in per.items():
            self.off[name] = (i - first) * by + self.off.get(name, 0)

    def leave(self, turns, per):
        n0, off0, bank0 = self.at_entry
        made = {name: n - n0.get(name, 0) for name, n in self.n.items() if n != n0.get(name, 0)}
        assert made == per, (made, per)
        for b, (name, n) in self.bank.items():
            assert bank0.get(b) in ((name, n), (name, n - per.get(name, 0))), (b, name)
        for name, by in per.items():
            self.off[name] = (turns - 1) * by + off0.get(name, 0)


def gnn_moe_stack(nc, a, out):
    with ExitStack() as ctx:
        def sb(name, shape, dt=F32):
            return ctx.enter_context(nc.sbuf_tensor(name, shape, dt))

        def sem(name):
            return ctx.enter_context(nc.semaphore(name))

        maskT = sb("maskT", [P, T, N], BF16)
        x = sb("x", [P, T, P])
        hT = sb("hT", [P, N])
        hTc = sb("hTc", [P, CW])
        xc = sb("xc", [P, CT, P])
        xn = sb("xn", [P, CT, P])
        sbc = sb("sbc", [P, H, CW])
        odiv = xc
        att = sb("att", [P, CT * 2 * VW])
        ysb = sb("ysb", [P, 3, CW])
        arena = sb("arena", [P, 12288])
        wnat = [arena[:, s * P:(s + 1) * P] for s in range(2)]
        brep = arena[:, 2 * P:3 * P]
        ind = arena[:, 0:8192].bitcast(BF16).rearrange("p (q b j i) -> p q b j i", q=Q, b=2, j=QT)
        uf = arena[:, 3 * P:3 * P + T * H * 2 * V1].rearrange("p (g v) -> p g v", v=V1)
        whx0 = arena[:, 8192:8192 + T * XC].rearrange("p (t k) -> p t k", t=T)
        w1 = arena[:, 8192:10240].rearrange("p (s e f) -> p s e f", s=2, e=2)
        w2 = arena[:, 10240:12288].rearrange("p (s e c d) -> p s e c d", s=2, e=2, c=HC)
        wsel = arena[:, 0:4096].rearrange("p (s k n) -> p s k n", s=L * GT, k=KC)
        at = [4096]

        def in_arena(parts, *dims):
            n = int(np.prod(dims))
            at[0] += n
            return arena[0:parts, at[0] - n:at[0]]

        wiT = in_arena(P, HID)
        bi = in_arena(P, KC)
        ws = in_arena(P, L, KC * HID).rearrange("p (l n) -> p l n", l=L)
        brs = in_arena(E1, L, HID).rearrange("p (l n) -> p l n", l=L)
        bsr = in_arena(E1, L, HID).rearrange("p (l n) -> p l n", l=L)
        woT = in_arena(P, KC, P).rearrange("p (k n) -> p k n", k=KC)
        bo = in_arena(1, P)
        htt = in_arena(P, 3, KC * P).rearrange("p (l n) -> p l n", l=3)
        reg_b = sb("reg_b", [P, T * H * 2 * VW // 2])
        u = reg_b[:, :].bitcast(BF16).rearrange("p (g s v) -> p g s v", s=PARTS, v=V1)
        v1 = reg_b[:, 0:T * (P + 1)].rearrange("p (t v) -> p t v", t=T)
        whx1 = reg_b[:, T * (P + 1):T * (P + 1) + T * XC].rearrange("p (t k) -> p t k", t=T)
        reg_c = sb("reg_c", [P, 4096])
        adj = reg_c[:, :].bitcast(BF16).rearrange("p (s j) -> p s j", s=4)
        hid = reg_c[:, :].rearrange("p (e c i) -> p e c i", e=2, c=HC)
        prob = reg_c[:, :].rearrange("p (s i) -> p s i", s=8)
        wxs = [sb(f"wx{s}", [P, XC]) for s in range(2)]
        asel = [sb(f"asel{s}", [P, 2 * H]) for s in range(2)]
        wrep = sb("wrep", [P, H, P])
        ident = sb("ident", [P, P])
        identb = sb("identb", [P, P], BF16)
        ones = sb("ones", [P, P])
        consts = sb("consts", [P, 5])
        bcol = sb("bcol", [P, 1])
        bx = sb("bx", [1, XC])
        bac = sb("bac", [P, 2 * H])
        nmean = sb("nmean", [P, CT])
        svar = sb("svar", [P, CT])
        sstd = sb("sstd", [P, CT])
        rstd = sb("rstd", [P, CT])
        nd = sb("nd", [P, T, H])
        dsh = sb("dsh", [P, T, H])
        dsum = sb("dsum", [P, T])
        bd = sb("bd", [P, T, H, 2])
        ab = sb("ab", [P, T, H, 2])
        arg = sb("arg", [P, T, H, 2])
        zt = sb("zt", [P, T, H])
        zm = sb("zm", [P, T, H])
        pmax = sb("pmax", [P, 5])
        gmax = sb("gmax", [P, 2, 5])
        nmx = sb("nmx", [P, 5])
        red = sb("red", [P, 2 * CT, V1])
        wred = sb("wred", [P, 2 * CT, V1])
        num = sb("num", [P, CT, V1])
        rden = sb("rden", [P, CT])
        wgT = sb("wgT", [P, E0])
        bg = sb("bg", [1, E0])
        b1 = sb("b1", [P, E0, HC])
        b2 = sb("b2", [E0, P])
        sc = sb("sc", [P, CT, E0])
        sc2 = sb("sc2", [P, CT, E0])
        first_i = sb("first_i", [P, E0], I32)
        first_w = sb("first_w", [P, E0])
        oh = sb("oh", [P, 2, CT, E0])
        key = sb("key", [P, CT, E0])
        gst = sb("gst", [P, 8, CT])
        comb = sb("comb", [P, CT, E0])
        ohx = sb("ohx", [E1, CW])
        combT = ohx[0:E0, :].rearrange("e (t i) -> e t i", t=CT)
        route = sb("route", [1, N // GRP], I32)
        route16 = sb("route16", [E1, N // GRP], I32)
        routef = sb("routef", [E1, N // GRP])
        chan_i = sb("chan_i", [E1, 1], I32)
        chan = sb("chan", [E1, 1])
        onehot = sb("onehot", [E1, N // GRP])

        bank = [ctx.enter_context(nc.psum_tensor(f"bank{b}", [P, 512], F32)) for b in range(8)]
        bankb = [t[:, :].bitcast(BF16) for t in bank]

        full = [sem(f"bank{b}_full") for b in range(8)]
        s_x = [sem(f"x_chunk{c}_loaded") for c in range(C)]
        s_w = sem("small_weights_loaded")
        s_wp = [sem(f"expert_pair_slot{r}_loaded") for r in range(2)]
        s_w1 = sem("second_mixture_loaded")
        s_adj = [sem(f"adj_slot{r}_loaded") for r in range(4)]
        s_sel = [sem(f"selected_weights_slot{r}_loaded") for r in range(L * GT)]
        s_const = sem("constants_ready")
        s_pool = sem("gpsimd_step_done")
        s_dve = sem("vector_step_done")
        s_brep = sem("bias_replicated")
        s_rep = sem("replicated_score_weights_ready")
        s_var = sem("chunk_variance_ready")
        s_std = sem("chunk_deviation_ready")
        s_xn = sem("chunk_normalised")
        s_pm = sem("partition_maxima_ready")
        s_gm = sem("global_maxima_ready")
        s_arg = sem("exponents_ready")
        s_exp = sem("exponentials_ready")
        s_u = sem("values_ready")
        s_g = sem("indicator_above_ready")
        s_ind = sem("indicator_quad_ready")
        s_indf = sem("indicator_quad_used")
        s_attf = sem("attention_sums_used")
        s_gap = sem("gate_gap_ready")
        s_gex = sem("gate_exp_ready")
        s_comb = sem("combine_weights_ready")
        s_acc = sem("weighted_output_added")
        s_step = sem("product_step_done")
        s_prob = sem("probability_tile_ready")
        s_probf = sem("probability_quad_used")
        s_wc = sem("shared_weights_summed")
        s_ohx = sem("onehot_chunk_ready")
        s_out = sem("output_stored")
        ev = {name: sem(what) for name, what in (
            ("ext", "score_weights_ready"), ("mask", "mask_half_row_ready"), ("hTc", "chunk_transposed"),
            ("proj", "projected_half_chunk_ready"), ("rows", "source_row_ready"), ("att", "attention_sums_ready"),
            ("sc", "gate_scores_ready"), ("combT", "combine_weights_transposed"), ("hid", "hidden_block_ready"),
            ("y", "weighted_output_ready"), ("htt", "hidden_tile_ready"))}
        NW = 4 + 2 * H + 8
        NW1 = 7
        NC = 8
        BANK3 = 2 * C + C * E0 * HC // 2
        FFN_Y = C * (E0 + 1)
        block = ctx.enter_context(nc.Block())

        def more(ap, n):
            return ap.unsqueeze(len(ap.shape)).to_broadcast([*ap.shape, n])

        @block.sync
        def _(sp):
            xin = a["x"].rearrange("(t p) d -> p t d", p=P)
            for c in range(C):
                sp.dma_start(x[:, c * CT:(c + 1) * CT, :], xin[:, c * CT:(c + 1) * CT, :]).then_inc(s_x[c], 16)
            sp.wait_ge(s_const, NC)
            with nc.allow_non_contiguous_dma(reason="small vectors"):
                for s in range(2):
                    sp.dma_start(wnat[s], a[f"gW{s}"]).then_inc(s_w, 16)
                    sp.dma_start(wxs[s][:, 0:P], a[f"gWT{s}"]).then_inc(s_w, 16)
                for h in range(H):
                    for s in range(2):
                        src = a["ga0"][h:h + 1, :] if s == 0 else a["ga1"]
                        sp.dma_start(asel[s][h * DH:(h + 1) * DH, h:2 * H:H],
                                     src.rearrange("o (k d) -> (o d) k", k=2)).then_inc(s_w, 16)
                sp.dma_start(bcol[:, :], a["gb0"].rearrange("o k -> k o")).then_inc(s_w, 16)
            sp.dma_start(bx[0:1, 0:P], a["gb0"]).then_inc(s_w, 16)
            sp.dma_start(wgT[:, :], a["wgT"]).then_inc(s_w, 16)
            sp.dma_start(bg[:, :], a["bg"]).then_inc(s_w, 16)
            sp.dma_start(b1[:, :, :], a["b1"]).then_inc(s_w, 16)
            sp.dma_start(b2[:, :], a["b2"]).then_inc(s_w, 16)
            sp.dma_start(route[:, :], a["route"]).then_inc(s_w, 16)
            sp.dma_start(route16[:, :], a["route"].to_broadcast([E1, N // GRP])).then_inc(s_w, 16)
            sp.wait_ge(s_u, 1)

            def load_pair(c, h, wait):
                if wait:
                    sp.wait_ge(full[5], c * (H + 1) + (h if h >= 2 else h - 1))
                e = slice(2 * h, 2 * h + 2)
                sp.dma_start(w1[:, h % 2, :, :], a["w1T"][:, e, :]).then_inc(s_wp[h % 2], 16)
                sp.dma_start(w2[:, h % 2, :, :, :], a["w2T"][:, e, :, :]).then_inc(s_wp[h % 2], 16)

            for h in range(H):
                load_pair(0, h, h >= 2)
            with sp.Fori(1, C) as c:
                for h in range(H):
                    load_pair(c, h, True)
            sp.wait_ge(s_acc, FFN_Y)
            sp.dma_start(wiT, a["wiT"]).then_inc(s_w1, 16)
            sp.dma_start(bi, a["bi"]).then_inc(s_w1, 16)
            sp.dma_start(ws, a["wsT"]).then_inc(s_w1, 16)
            sp.dma_start(brs, a["br"]).then_inc(s_w1, 16)
            sp.dma_start(bsr, a["bs"].to_broadcast([E1, L, HID])).then_inc(s_w1, 16)
            sp.dma_start(woT, a["woT"]).then_inc(s_w1, 16)
            sp.dma_start(bo, a["bo"]).then_inc(s_w1, 16)

            def select(t, wait):
                for l in range(L):
                    for g in range(GT):
                        s = l * GT + g
                        e = sp.value_load(route[0:1, bass.ds(t * GT + g, 1)], min_val=0, max_val=E1 - 1)
                        if wait:
                            sp.wait_ge(full[3], (t - 1) * L + (BANK3 + l + 1))
                        sp.dma_start(wsel[:, s, :, :].rearrange("p k n -> p (k n)").unsqueeze(1),
                                     a["wrT"][:, l, bass.ds(e, 1), :]).then_inc(s_sel[s], 16)

            select(0, False)
            with sp.Fori(1, T) as t:
                select(t, True)

        @block.gpsimd
        def _(pool):
            nc.gpsimd.memset(ident[:, :], 0.0).then_inc(s_pool, 1)
            for m in (asel[0], asel[1]):
                nc.gpsimd.memset(m[:, :], 0.0).then_inc(s_const, 1)
            nc.gpsimd.memset(ones[:, :], 1.0).then_inc(s_const, 1)
            for i, v in enumerate((EPS, SHIFT, SLOPE * SHIFT, -SHIFT, -SLOPE * SHIFT)):
                last = nc.gpsimd.memset(consts[:, i:i + 1], v)
            last.then_inc(s_const, 1)
            nc.gpsimd.iota(first_i[:, :], pattern=[[-1, E0]], base=E0, channel_multiplier=0).then_inc(s_pool, 1)
            nc.gpsimd.iota(chan_i[:, :], pattern=[[0, 1]], base=0, channel_multiplier=1).then_inc(s_pool, 1)
            pool.wait_ge(s_pool, 3)
            nc.gpsimd.affine_select(out=ident[:, :], in_=ident[:, :], compare_op=ALU.not_equal, fill=1.0,
                                    base=0, pattern=[[-1, P]], channel_multiplier=1).then_inc(s_pool, 1)
            nc.gpsimd.tensor_copy(first_w[:, :], first_i[:, :]).then_inc(s_const, 1)
            nc.gpsimd.tensor_copy(chan[:, :], chan_i[:, :]).then_inc(s_const, 1)
            pool.wait_ge(s_pool, 4)
            nc.gpsimd.tensor_copy(identb[:, :], ident[:, :]).then_inc(s_const, 1)
            nc.gpsimd.memset(pmax[:, :], 0.0).then_inc(s_const, 1)

            def load_rows(r):
                if r >= 4:
                    pool.wait_ge(full[7], r - 3 + (2 if r >= 8 else 0))
                pool.dma_start(adj[:, r % 4, :], a["adj"][r * P:(r + 1) * P, :]).then_inc(s_adj[r % 4], 16)

            for r in range(8):
                load_rows(r)
            pool.wait_ge(s_pm, 1)
            nc.gpsimd.partition_all_reduce(gmax[:, 0, :], pmax[:, :], P, RMAX).then_inc(s_gm, 1)
            for r in range(8, T):
                load_rows(r)

            for n in range(FFN_Y):
                c, e = divmod(n, E0 + 1)
                pool.wait_ge(ev["y"], n + 1)
                if e:
                    pool.wait_ge(s_acc, n)
                xi = x[:, c * CT:(c + 1) * CT, :]
                nc.gpsimd.tensor_tensor(xi, xi, ysb[:, e % 3, :].rearrange("p (t d) -> p t d", d=P),
                                        ALU.add).then_inc(s_acc, 1)
            pool.wait_ge(s_w, 16 * NW)
            nc.gpsimd.tensor_copy(routef[:, :], route16[:, :]).then_inc(s_pool, 1)
            pool.wait_ge(s_pool, 5)
            nc.gpsimd.tensor_scalar(onehot[:, :], routef[:, :], chan[:, 0:1], None,
                                    ALU.is_equal).then_inc(s_pool, 1)
            pool.wait_ge(s_w1, 16 * NW1)
            nc.gpsimd.tensor_tensor(brs, brs, bsr, ALU.add).then_inc(s_wc, 1)
            for l in range(L):
                for kc in range(KC):
                    d = ws[:, l, kc * HID + kc * P:kc * HID + (kc + 1) * P]
                    nc.gpsimd.tensor_tensor(d, d, ident[:, :], ALU.add).then_inc(s_wc, 1)
            pool.wait_ge(s_pm, 2)
            nc.gpsimd.partition_all_reduce(gmax[:, 1, :], pmax[:, :], P, RMAX).then_inc(s_gm, 1)
            pool.wait_ge(s_pool, 6)
            outv = out.rearrange("(t p) d -> p t d", p=P)
            for c in range(C):
                nc.gpsimd.tensor_copy(ohx[:, :].rearrange("e (g i) -> e g i", i=GRP),
                                      more(onehot[:, c * CT * GT:(c + 1) * CT * GT], GRP)).then_inc(s_ohx, 1)
                for i in range(CT):
                    pool.wait_ge(ev["y"], FFN_Y + c * CT + i + 1)
                    xi = x[:, c * CT + i, :]
                    nc.gpsimd.tensor_tensor(xi, xi, ysb[:, 0, i * P:(i + 1) * P], ALU.add).then_inc(s_acc, 1)
                pool.wait_ge(s_acc, FFN_Y + c * CT + CT)
                pool.dma_start(outv[:, c * CT:(c + 1) * CT, :],
                               x[:, c * CT:(c + 1) * CT, :]).then_inc(s_out, 16)
            pool.wait_ge(s_out, 16 * C)

        @block.tensor
        def _(pe):
            k = Count()
            mm = nc.tensor.matmul

            def use(b, event):
                if b in k.bank:
                    name, v = k.freed(b)
                    pe.wait_ge(ev[name], v)
                k.fill(b, event)

            def ln_transpose():
                pe.wait_ge(s_xn, k.event("xn"))
                use(6, "hTc")
                for i in range(CT):
                    last = nc.tensor.transpose(bank[6][:, i * P:(i + 1) * P], xn[:, i, :], ident[:, :])
                last.then_inc(full[6], 1)
                pe.wait_ge(ev["hTc"], k.at("hTc"))

            def mask_rows(r):
                pe.wait_ge(s_adj[r % 4], 16 * (r // 4 + 1))
                for half in range(2):
                    b = 6 + half
                    use(b, "mask")
                    for j in range(T // 2):
                        jt = half * T // 2 + j
                        last = nc.tensor.transpose(bankb[b][:, j * P:(j + 1) * P],
                                                   adj[:, r % 4, jt * P:(jt + 1) * P], identb[:, :])
                    last.then_inc(full[b], 1)

            def project(s):
                for i in range(CT):
                    b = 2 + i // 2
                    if i % 2 == 0:
                        use(b, "proj")
                    o = bank[b][:, (i % 2) * XC:(i % 2 + 1) * XC]
                    last = mm(o, hTc[:, i * P:(i + 1) * P], wxs[s][:, :], start=True, stop=(s == 1))
                    if s == 0:
                        last = mm(o, ones[0:1, :], bx[:, :], start=False, stop=True)
                    if i % 2:
                        last.then_inc(full[b], 1)

            def source_rows(s, c):
                for h in range(H):
                    b = 6 + h % 2
                    use(b, "rows")
                    mm(bank[b][:, :], wrep[:, h, :], hT[:, bass.ts(c, CW)], start=True,
                       stop=True).then_inc(full[b], 1)

            def attend(h):
                use(0, "att")
                use(1, "att")
                for q in range(Q):
                    pe.wait_ge(s_ind, k.event("ind"))
                    for j in range(QT):
                        t = q * QT + j
                        for i in range(CT):
                            for b in range(2):
                                o = (i % 2) * 2 * VW + b * VW
                                last = mm(bank[i // 2][:, o:o + VW], ind[:, q, b, j, i * P:(i + 1) * P],
                                          u[:, (t * H + h) * 2 + b, :, :],
                                          start=(t == 0 and i % 2 == 0 and b == 0), stop=(t == T - 1),
                                          skip_group_check=True)
                            if t == T - 1 and i % 2:
                                last.then_inc(full[i // 2], 1)
                    if q < Q - 1:
                        last.then_inc(s_indf, 1)

            def gate():
                ln_transpose()
                use(4, "sc")
                for i in range(CT):
                    o = bank[4][:, i * E0:(i + 1) * E0]
                    mm(o, hTc[:, i * P:(i + 1) * P], wgT[:, :], start=True, stop=False)
                    last = mm(o, ones[0:1, :], bg[:, :], start=False, stop=True)
                last.then_inc(full[4], 1)
                pe.wait_ge(s_comb, k.event("comb"))
                use(6, "combT")
                for i in range(CT):
                    last = nc.tensor.transpose(bank[6][0:E0, i * P:(i + 1) * P], comb[:, i, :], ident[:, :])
                last.then_inc(full[6], 1)
                pe.wait_ge(ev["combT"], k.at("combT"))
                use(5, "y")
                for i in range(CT):
                    last = mm(bank[5][:, i * P:(i + 1) * P], combT[:, i, :], b2[:, :], start=True, stop=True)
                last.then_inc(full[5], 1)

            def experts(pair):
                s = pair % 2
                pe.wait_ge(s_wp[s], k.event(f"pair{s}", 32))
                for e in (2 * pair, 2 * pair + 1):
                    for c in range(HC):
                        b = 2 + c % 2
                        use(b, "hid")
                        mm(bank[b][:, :], w1[:, s, e % 2, c * P:(c + 1) * P], hTc[:, :], start=True,
                           stop=True).then_inc(full[b], 1)
                for e in (2 * pair, 2 * pair + 1):
                    b = 4 + e % 2
                    use(b, "y")
                    pe.wait_ge(ev["hid"], k.at("hid") - (HC if e % 2 == 0 else 0))
                    for i in range(CT):
                        for c in range(HC):
                            last = mm(bank[b][:, i * P:(i + 1) * P], hid[:, e % 2, c, i * P:(i + 1) * P],
                                      w2[:, s, e % 2, c, :], start=(c == 0), stop=(c == HC - 1))
                    last.then_inc(full[b], 1)

            pe.wait_ge(s_w, 16 * NW)
            pe.wait_ge(s_const, NC)
            pe.wait_ge(s_brep, 1)
            use(6, "ext")
            mm(bank[6][:, 0:8], wnat[0], asel[0][:, :], start=True, stop=True)
            mm(bank[6][:, 8:16], wnat[1], asel[1][:, :], start=True, stop=True)
            mm(bank[6][:, 16:24], brep, asel[0][:, :], start=True, stop=True)
            mm(bank[6][0:1, 24:32], bcol[:, :], asel[0][:, :], start=True, stop=True).then_inc(full[6], 1)
            for r in range(CT):
                mask_rows(r)
            per = {"xn": 1, "hTc": 1, "proj": 2}
            ln_transpose()
            project(0)
            with pe.Fori(1, C) as c:
                k.enter(c, 1, per)
                ln_transpose()
                project(0)
                k.leave(C - 1, per)
            pe.wait_ge(s_rep, H)
            source_rows(0, 0)
            pe.wait_ge(s_u, 1)
            for h in range(H):
                attend(h)
                for r in range(CT + 3 * h, CT + 3 * h + 3):
                    mask_rows(r)
            source_rows(0, 1)

            def chunk0(c, next_rows):
                for h in range(H):
                    attend(h)
                    if h == H - 1:
                        source_rows(0, next_rows)
                    if h == 0:
                        gate()
                    experts(h)

            chunk0(1, 2)
            per = {"att": 8, "ind": 16, "rows": 4, "xn": 1, "hTc": 1, "sc": 1, "comb": 1, "combT": 1,
                   "hid": 32, "y": 9, "pair0": 64, "pair1": 64}
            with pe.Fori(2, C) as c:
                k.enter(c, 2, per)
                chunk0(c, (c + 1) % C)
                k.leave(C - 2, per)
            gate()
            for h in range(H):
                experts(h)

            per = {"xn": 1, "hTc": 1, "proj": 2}
            ln_transpose()
            project(1)
            with pe.Fori(1, C) as c:
                k.enter(c, 1, per)
                ln_transpose()
                project(1)
                k.leave(C - 1, per)
            pe.wait_ge(s_rep, 2 * H)
            source_rows(1, 0)
            pe.wait_ge(s_u, 2)

            def attend1(q):
                if q == 0:
                    use(0, "att")
                    use(1, "att")
                for j in range(QT):
                    pe.wait_ge(s_prob, k.event("prob"))
                    t = q * QT + j
                    for i in range(CT):
                        b, o = (0, i * (P + 1)) if i < 3 else (1, 0)
                        last = mm(bank[b][:, o:o + P + 1], prob[:, t % 8, i * P:(i + 1) * P], v1[:, t, :],
                                  start=(t == 0 and i in (0, 3)), stop=(t == T - 1), skip_group_check=True)
                        if t == T - 1 and i >= 2:
                            last.then_inc(full[b], 1)
                if q < Q - 1:
                    last.then_inc(s_probf, 1)

            def tile1(i):
                use(2, "htt")
                for m in range(KC):
                    last = mm(bank[2][:, m * P:(m + 1) * P], wiT[:, m * P:(m + 1) * P],
                              hTc[:, i * P:(i + 1) * P], start=True, stop=True)
                last.then_inc(full[2], 1)
                k.event("tile")
                for l in range(L):
                    pe.wait_ge(ev["htt"], k.at("htt"))
                    use(3, "htt")
                    for m in range(KC):
                        mm(bank[3][:, m * P:(m + 1) * P], brs[:, l, m * P:(m + 1) * P],
                           ohx[:, i * P:(i + 1) * P], start=(m == 0), stop=False, skip_group_check=True)
                        for kc in range(KC):
                            mm(bank[3][:, m * P:(m + 1) * P],
                               ws[:, l, kc * HID + m * P:kc * HID + (m + 1) * P], htt[:, l, kc * P:(kc + 1) * P],
                               start=False, stop=False, skip_group_check=True)
                    for g in range(GT):
                        pe.wait_ge(s_sel[l * GT + g], k.at("tile") * 16)
                        for m in range(KC):
                            for kc in range(KC):
                                o = m * P + g * GRP
                                last = mm(bank[3][:, o:o + GRP], wsel[:, l * GT + g, kc, m * P:(m + 1) * P],
                                          htt[:, l, kc * P + g * GRP:kc * P + (g + 1) * GRP],
                                          start=False, stop=(kc == KC - 1), skip_group_check=True)
                    last.then_inc(full[3], 1)
                pe.wait_ge(ev["htt"], k.at("htt"))
                use(4, "y")
                for kc in range(KC):
                    mm(bank[4][:, 0:P], htt[:, 2, kc * P:(kc + 1) * P], woT[:, kc, :], start=(kc == 0), stop=False)
                mm(bank[4][:, 0:P], ones[0:1, :], bo[:, :], start=False, stop=True).then_inc(full[4], 1)

            for q in range(Q):
                attend1(q)
            source_rows(1, 1)
            pe.wait_ge(s_wc, 1 + L * KC)

            def chunk1(next_rows):
                for q in range(Q):
                    attend1(q)
                    if q == Q - 1:
                        source_rows(1, next_rows)
                    if q == 0:
                        ln_transpose()
                        pe.wait_ge(s_ohx, k.event("ohx"))
                    tile1(q)

            chunk1(2)
            per = {"att": 2, "prob": 16, "rows": 4, "xn": 1, "hTc": 1, "ohx": 1, "tile": 4, "htt": 12, "y": 4}
            with pe.Fori(2, C) as c:
                k.enter(c, 2, per)
                chunk1((c + 1) % C)
                k.leave(C - 2, per)
            ln_transpose()
            pe.wait_ge(s_ohx, k.event("ohx"))
            for q in range(Q):
                tile1(q)

        @block.scalar
        def _(act):
            k = Count()
            af = nc.scalar.activation

            def got(b):
                act.wait_ge(full[b], k.event(f"full{b}"))

            def ln_std():
                act.wait_ge(s_var, k.event("var"))
                af(sstd[:, :], svar[:, :], ACT.Sqrt, bias=consts[:, 0:1], scale=1.0 / P).then_inc(s_std, 1)

            def ln_out(c=None):
                got(6)
                if c is not None:
                    af(hT[:, bass.ts(c, CW)], bank[6][:, :], ACT.Copy)
                af(hTc[:, :], bank[6][:, :], ACT.Copy).then_inc(ev["hTc"], 1)

            def mask_rows(r):
                for half in range(2):
                    b = 6 + half
                    got(b)
                    af(maskT[:, half * 8:(half + 1) * 8, r * P:(r + 1) * P],
                       bankb[b].rearrange("p (j i) -> p j i", i=P), ACT.Copy).then_inc(ev["mask"], 1)

            def project(whx, c):
                for half in range(2):
                    b = 2 + half
                    got(b)
                    af(whx[:, bass.ds(c * CT + 2 * half, 2), :],
                       bank[b][:, 0:2 * XC].rearrange("p (t k) -> p t k", t=2), ACT.Copy).then_inc(ev["proj"], 1)

            def source_rows(s):
                for h in range(H):
                    b = 6 + h % 2
                    got(b)
                    if s == 0:
                        af(sbc[:, h, :], bank[b][:, :], ACT.Copy).then_inc(ev["rows"], 1)
                    else:
                        af(sbc[:, h, :], bank[b][:, :], ACT.Exp, bias=nmx[:, h:h + 1],
                           scale=SLOPE).then_inc(ev["rows"], 1)

            def sums(*widths):
                v = k.event("sums") - 1
                if not (isinstance(v, int) and v <= 0):
                    act.wait_ge(s_attf, v)
                o = 0
                for b, w in enumerate(widths):
                    got(b)
                    af(att[:, o:o + w], bank[b][:, 0:w], ACT.Copy).then_inc(ev["att"], 1)
                    o += w

            def y_slot(slots):
                v = k.event("y") - slots
                if not (isinstance(v, int) and v <= 0):
                    act.wait_ge(s_acc, v)

            def gate():
                ln_std()
                ln_out()
                got(4)
                af(sc[:, :, :], bank[4][:, 0:CT * E0].rearrange("p (t e) -> p t e", e=E0),
                   ACT.Copy).then_inc(ev["sc"], 1)
                act.wait_ge(s_gap, k.event("gap"))
                af(gst[:, 3, :], gst[:, 2, :], ACT.Exp).then_inc(s_gex, 1)
                got(6)
                af(combT[:, :, :], bank[6][0:E0, :].rearrange("p (t i) -> p t i", i=P),
                   ACT.Copy).then_inc(ev["combT"], 1)
                y_slot(3)
                got(5)
                af(ysb[:, 0, :], bank[5][:, :], ACT.Copy).then_inc(ev["y"], 1)

            def experts(pair):
                for e in (2 * pair, 2 * pair + 1):
                    for c in range(HC):
                        got(2 + c % 2)
                        af(hid[:, e % 2, c, :], bank[2 + c % 2][:, :], ACT.Relu,
                           bias=b1[:, e, c:c + 1]).then_inc(ev["hid"], 1)
                for e in (2 * pair, 2 * pair + 1):
                    y_slot(3)
                    got(4 + e % 2)
                    for i in range(CT):
                        last = af(ysb[:, (e + 1) % 3, i * P:(i + 1) * P],
                                  bank[4 + e % 2][:, i * P:(i + 1) * P], ACT.Copy, scale=comb[:, i, e:e + 1])
                    last.then_inc(ev["y"], 1)

            got(6)
            af(wxs[0][:, P:XC], bank[6][:, 0:8], ACT.Copy)
            af(wxs[1][:, P:XC], bank[6][:, 8:16], ACT.Copy)
            af(bac[:, :], bank[6][:, 16:24], ACT.Copy)
            af(bx[0:1, P:XC], bank[6][0:1, 24:32], ACT.Copy).then_inc(ev["ext"], 1)
            for r in range(CT):
                mask_rows(r)

            def prelude(whx):
                per = {"var": 1, "full6": 1, "full2": 1, "full3": 1}
                with act.Fori(0, C) as c:
                    k.enter(c, 0, per)
                    ln_std()
                    ln_out(c)
                    project(whx, c)
                    k.leave(C, per)

            prelude(whx0)
            act.wait_ge(s_arg, 1)
            af(bd[:, :, :, 0], dsh[:, :, :], ACT.Exp, bias=consts[:, 1:2])
            af(bd[:, :, :, 1], dsh[:, :, :], ACT.Exp, bias=consts[:, 2:3], scale=SLOPE).then_inc(s_exp, 1)
            act.wait_ge(s_arg, 2)
            af(ab[:, :, :, 0], arg[:, :, :, 0], ACT.Exp, bias=consts[:, 3:4])
            af(ab[:, :, :, 1], arg[:, :, :, 1], ACT.Exp, bias=consts[:, 4:5]).then_inc(s_exp, 1)
            source_rows(0)
            for h in range(H):
                sums(4 * VW, 4 * VW)
                for r in range(CT + 3 * h, CT + 3 * h + 3):
                    mask_rows(r)
            source_rows(0)
            per = {"sums": 4, "full0": 4, "full1": 4, "full6": 4, "full7": 2, "var": 1, "full4": 5, "gap": 1,
                   "full5": 5, "y": 9, "full2": 16, "full3": 16}

            def chunk0():
                for h in range(H):
                    sums(4 * VW, 4 * VW)
                    if h == H - 1:
                        source_rows(0)
                    if h == 0:
                        gate()
                    experts(h)

            chunk0()
            with act.Fori(2, C) as c:
                k.enter(c, 2, per)
                chunk0()
                k.leave(C - 2, per)
            gate()
            for h in range(H):
                experts(h)

            prelude(whx1)
            act.wait_ge(s_arg, 3)
            for h in range(H):
                af(nd[:, :, h], whx1[:, :, P + H + h], ACT.Exp, bias=nmx[:, h:h + 1], scale=-SLOPE)
            af(v1[:, :, P], dsum[:, :], ACT.Exp, bias=nmx[:, 4:5], scale=1.0 / H).then_inc(s_exp, 1)
            source_rows(1)
            sums(3 * (P + 1), P + 1)
            source_rows(1)

            def tile1(i):
                got(2)
                for m in range(KC):
                    last = af(htt[:, 0, m * P:(m + 1) * P], bank[2][:, m * P:(m + 1) * P], ACT.Relu,
                              bias=bi[:, m:m + 1])
                last.then_inc(ev["htt"], 1)
                for l in range(L):
                    got(3)
                    af(htt[:, l + 1, :], bank[3][:, 0:KC * P], ACT.Relu).then_inc(ev["htt"], 1)
                y_slot(CT)
                got(4)
                af(ysb[:, 0, i * P:(i + 1) * P], bank[4][:, 0:P], ACT.Copy).then_inc(ev["y"], 1)

            per = {"sums": 1, "full0": 1, "full1": 1, "full6": 3, "full7": 2, "var": 1, "full2": 4, "full3": 8,
                   "full4": 4, "y": 4}
            with act.Fori(1, C) as c:
                k.enter(c, 1, per)
                for q in range(Q):
                    if q == Q - 1:
                        sums(3 * (P + 1), P + 1)
                        source_rows(1)
                    if q == 0:
                        ln_std()
                        ln_out()
                    tile1(q)
                k.leave(C - 1, per)
            ln_std()
            ln_out()
            for q in range(Q):
                tile1(q)

        @block.vector
        def _(dve):
            k = Count()
            v = nc.vector

            def then(ins):
                ins.then_inc(s_dve, 1)
                dve.wait_ge(s_dve, k.event("dve"))

            def norm(c, unit):
                xi = x[:, bass.ts(c, CT), :]
                then(v.tensor_scalar(xc[:, :, :], xi, -1.0 / P, None, ALU.mult))
                then(v.reduce_sum(nmean[:, :], xc[:, :, :], AX_X))
                then(v.tensor_tensor(xc[:, :, :], xi, more(nmean[:, :], P), ALU.add))
                if not (isinstance(unit, int) and unit == 0):
                    dve.wait_ge(ev["hTc"], unit)
                then(v.tensor_tensor(xn[:, :, :], xc[:, :, :], xc[:, :, :], ALU.mult))
                v.reduce_sum(svar[:, :], xn[:, :, :], AX_X).then_inc(s_var, 1)
                dve.wait_ge(s_std, unit + 1)
                then(v.reciprocal(rstd[:, :], sstd[:, :]))
                v.tensor_tensor(xn[:, :, :], xc[:, :, :], more(rstd[:, :], P), ALU.mult).then_inc(s_xn, 1)
                dve.wait_ge(s_xn, unit + 1)

            dve.wait_ge(s_const, NC)
            dve.wait_ge(s_w, 16 * NW)
            v.tensor_scalar(brep, ones[:, :], bcol[:, 0:1], None, ALU.mult).then_inc(s_brep, 1)
            dve.wait_ge(ev["ext"], 1)
            def replicate(s):
                for h in range(H):
                    v.tensor_scalar(wrep[:, h, :], ones[:, :], wxs[s][:, P + h:P + h + 1], None,
                                    ALU.mult).then_inc(s_rep, 1)

            replicate(0)
            for c in range(C):
                dve.wait_ge(s_x[c], 16)

            def norms(unit0):
                with dve.Fori(0, C) as c:
                    k.enter(c, 0, {"dve": 5})
                    norm(c, c + unit0)
                    k.leave(C, {"dve": 5})

            def norms_first():
                norm(0, 0)
                with dve.Fori(1, C) as c:
                    k.enter(c, 1, {"dve": 5})
                    norm(c, c)
                    k.leave(C - 1, {"dve": 5})

            norms_first()

            dve.wait_ge(ev["proj"], 2 * C)
            S0, D0 = whx0[:, :, P:P + H], whx0[:, :, P + H:P + 2 * H]
            v.scalar_tensor_tensor(nd[:, :, :], D0, -1.0,
                                   bac[:, 0:H].unsqueeze(1).to_broadcast([P, T, H]), ALU.mult, ALU.subtract)
            v.tensor_reduce(pmax[:, 0:H], D0.rearrange("p t h -> p h t"), AX_X, ALU.max).then_inc(s_pm, 1)
            dve.wait_ge(s_gm, 1)
            g0 = gmax[:, 0, 0:H].unsqueeze(1).to_broadcast([P, T, H])
            v.tensor_tensor(dsh[:, :, :], D0, g0, ALU.subtract).then_inc(s_arg, 1)
            then(v.tensor_tensor(zt[:, :, :], S0, g0, ALU.add))
            then(v.scalar_tensor_tensor(zm[:, :, :], zt[:, :, :], SLOPE, zt[:, :, :], ALU.mult, ALU.max))
            v.tensor_tensor(arg[:, :, :, 0], zt[:, :, :], zm[:, :, :], ALU.subtract)
            v.scalar_tensor_tensor(arg[:, :, :, 1], zt[:, :, :], SLOPE, zm[:, :, :], ALU.mult,
                                   ALU.subtract).then_inc(s_arg, 1)
            dve.wait_ge(s_exp, 1)
            uf4 = uf.rearrange("p (t h b) v -> p t h b v", t=T, h=H)
            for b in range(2):
                v.tensor_tensor(uf4[:, :, :, b, 0:DH], whx0[:, :, 0:P].rearrange("p t (h d) -> p t h d", h=H),
                                more(bd[:, :, :, b], DH), ALU.mult)
            then(v.tensor_copy(uf[:, :, DH], bd[:, :, :, :].rearrange("p t h b -> p (t h b)")))
            then(v.tensor_copy(u[:, :, 0, :], uf))
            then(v.tensor_tensor(uf, uf, u[:, :, 0, :], ALU.subtract))
            then(v.tensor_copy(u[:, :, 1, :], uf))
            v.tensor_tensor(u[:, :, 2, :], uf, u[:, :, 1, :], ALU.subtract).then_inc(s_u, 1)

            def indicate(c, h):
                n = c * H + h
                cs = bass.ts(c, CW)
                for q in range(Q):
                    if not (isinstance(n, int) and n == 0):
                        if q < Q - 1:
                            dve.wait_ge(s_indf, n * (Q - 1) + (q + 1 - (Q - 1)))
                        else:
                            dve.wait_ge(full[1], n)
                    for j in range(QT):
                        t = q * QT + j
                        last = v.scalar_tensor_tensor(ind[:, q, 0, j, :], sbc[:, h, :], nd[:, t, h:h + 1],
                                                      maskT[:, t, cs], ALU.is_gt, ALU.mult)
                    last.then_inc(s_g, 1)
                    dve.wait_ge(s_g, n * Q + (q + 1))
                    v.tensor_tensor(ind[:, q, 1, :, :], maskT[:, q * QT:(q + 1) * QT, cs], ind[:, q, 0, :, :],
                                    ALU.subtract).then_inc(s_ind, 1)

            def merge(c, h):
                n = c * H + h
                dve.wait_ge(ev["att"], n * 2 + 2)
                a4 = att[:, :].rearrange("p (g s v) -> p g s v", s=PARTS, v=V1)
                then(v.tensor_tensor(red[:, :, :], a4[:, :, 1, :], a4[:, :, 2, :], ALU.add))
                v.tensor_tensor(red[:, :, :], red[:, :, :], a4[:, :, 0, :], ALU.add).then_inc(s_attf, 1)
                dve.wait_ge(s_attf, n + 1)
                dve.wait_ge(s_exp, 2)
                then(v.tensor_tensor(wred[:, :, :].rearrange("p (t b) v -> p t b v", b=2),
                                     red[:, :, :].rearrange("p (t b) v -> p t b v", b=2),
                                     more(ab[:, bass.ts(c, CT), h, :], V1), ALU.mult))
                w4 = wred[:, :, :].rearrange("p (t b) v -> p t b v", b=2)
                then(v.tensor_tensor(num[:, :, :], w4[:, :, 0, :], w4[:, :, 1, :], ALU.add))
                then(v.reciprocal(rden[:, :], num[:, :, DH]))
                then(v.tensor_tensor(odiv[:, :, 0:DH], num[:, :, 0:DH], more(rden[:, :], DH), ALU.mult))
                xo = x[:, bass.ts(c, CT), h * DH:(h + 1) * DH]
                then(v.tensor_tensor(xo, xo, odiv[:, :, 0:DH], ALU.add))

            def gate(c, unit):
                norm(c, unit)
                dve.wait_ge(ev["sc"], unit - C + 1)
                fw = first_w[:, :].unsqueeze(1).to_broadcast([P, CT, E0])
                src = sc
                for r in range(2):
                    then(v.tensor_reduce(gst[:, r, :], src[:, :, :], AX_X, ALU.max))
                    then(v.tensor_tensor(key[:, :, :], src[:, :, :], more(gst[:, r, :], E0), ALU.is_equal))
                    then(v.tensor_tensor(key[:, :, :], key[:, :, :], fw, ALU.mult))
                    then(v.tensor_reduce(gst[:, 4, :], key[:, :, :], AX_X, ALU.max))
                    then(v.tensor_tensor(oh[:, r, :, :], key[:, :, :], more(gst[:, 4, :], E0), ALU.is_equal))
                    if r == 0:
                        then(v.scalar_tensor_tensor(sc2[:, :, :], oh[:, 0, :, :], NEG, sc[:, :, :], ALU.mult,
                                                    ALU.add))
                        src = sc2
                v.tensor_tensor(gst[:, 2, :], gst[:, 1, :], gst[:, 0, :], ALU.subtract).then_inc(s_gap, 1)
                dve.wait_ge(s_gex, unit - C + 1)
                then(v.tensor_scalar(gst[:, 5, :], gst[:, 3, :], 1.0, None, ALU.add))
                then(v.reciprocal(gst[:, 6, :], gst[:, 5, :]))
                then(v.tensor_tensor(gst[:, 7, :], gst[:, 3, :], gst[:, 6, :], ALU.mult))
                v.tensor_tensor(key[:, :, :], oh[:, 1, :, :], more(gst[:, 7, :], E0), ALU.mult)
                then(v.tensor_tensor(sc2[:, :, :], oh[:, 0, :, :], more(gst[:, 6, :], E0), ALU.mult))
                v.tensor_tensor(comb[:, :, :], key[:, :, :], sc2[:, :, :], ALU.add).then_inc(s_comb, 1)

            dve.wait_ge(ev["mask"], 2 * CT)
            dve.wait_ge(ev["rows"], H)
            dve.wait_ge(s_u, 1)
            for h in range(H):
                indicate(0, h)
                if h:
                    merge(0, h - 1)
            dve.wait_ge(ev["mask"], 2 * T)
            per = {"dve": 4 * 6 + 5 + 11 + 3 + 1}
            with dve.Fori(1, C) as c:
                k.enter(c, 1, per)
                dve.wait_ge(ev["rows"], c * H + H)
                indicate(c, 0)
                merge(c - 1, H - 1)
                gate(c - 1, c - 1 + C)
                for h in range(1, H):
                    indicate(c, h)
                    merge(c, h - 1)
                k.leave(C - 1, per)
            merge(C - 1, H - 1)
            gate(C - 1, 2 * C - 1)

            dve.wait_ge(s_acc, FFN_Y)
            replicate(1)
            norms(2 * C)
            dve.wait_ge(ev["proj"], 4 * C)
            S1, D1 = whx1[:, :, P:P + H], whx1[:, :, P + H:P + 2 * H]
            v.reduce_sum(dsum[:, :], D1, AX_X)
            then(v.scalar_tensor_tensor(zt[:, :, :], D1, -1.0, S1, ALU.mult, ALU.max))
            v.tensor_reduce(pmax[:, H:H + 1], dsum[:, :], AX_X, ALU.max)
            v.tensor_reduce(pmax[:, 0:H], zt[:, :, :].rearrange("p t h -> p h t"), AX_X,
                            ALU.max).then_inc(s_pm, 1)
            dve.wait_ge(s_gm, 2)
            v.tensor_scalar(nmx[:, 0:H], gmax[:, 1, 0:H], -SLOPE, None, ALU.mult)
            v.tensor_scalar(nmx[:, H:H + 1], gmax[:, 1, H:H + 1], -1.0 / H, None, ALU.mult).then_inc(s_arg, 1)
            dve.wait_ge(s_exp, 3)
            v.tensor_tensor(v1[:, :, 0:P], whx1[:, :, 0:P], v1[:, :, P:P + 1].to_broadcast([P, T, P]),
                            ALU.mult).then_inc(s_u, 1)

            def probabilities(c, first):
                cs = bass.ts(c, CW)
                for q in range(Q):
                    if q >= 2:
                        dve.wait_ge(s_probf, c * (Q - 1) + (q - 1))
                    elif not first:
                        if q == 0:
                            dve.wait_ge(s_probf, c * (Q - 1))
                        else:
                            dve.wait_ge(full[1], c + C * H)
                    for h in range(H):
                        for j in range(QT):
                            t = q * QT + j
                            if h:
                                dve.wait_ge(s_step, c * (T * (H - 1)) + (q * QT * (H - 1) + (h - 1) * QT + j + 1))
                            last = v.scalar_tensor_tensor(
                                prob[:, t % 8, :], sbc[:, h, :], nd[:, t, h:h + 1],
                                maskT[:, t, cs] if h == 0 else prob[:, t % 8, :], ALU.max, ALU.mult)
                            last.then_inc(s_step if h < H - 1 else s_prob, 1)

            def merge1(c):
                dve.wait_ge(ev["att"], c * 2 + (2 * C * H + 2))
                a3 = att[:, 0:CT * (P + 1)].rearrange("p (t v) -> p t v", v=P + 1)
                then(v.reciprocal(rden[:, :], a3[:, :, P]))
                v.tensor_tensor(odiv[:, :, :], a3[:, :, 0:P], more(rden[:, :], P), ALU.mult).then_inc(s_attf, 1)
                dve.wait_ge(s_attf, c + (C * H + 1))
                xo = x[:, bass.ts(c, CT), :]
                then(v.tensor_tensor(xo, xo, odiv[:, :, :], ALU.add))

            dve.wait_ge(ev["rows"], H * (C + 2))
            probabilities(0, True)
            per = {"dve": 7}
            with dve.Fori(1, C) as c:
                k.enter(c, 1, per)
                merge1(c - 1)
                norm(c - 1, c - 1 + 3 * C)
                dve.wait_ge(ev["rows"], c * H + H * (C + 2))
                probabilities(c, False)
                k.leave(C - 1, per)
            merge1(C - 1)
            norm(C - 1, 4 * C - 1)


def kernel(**inputs):
    import concourse.bacc as bacc
    from concourse.bass_utils import run_bass_kernel_spmd

    w = {n: np.asarray(v) for n, v in inputs.items()}
    lay = {
        "x": w["x"], "adj": w["adj"],
        "gW0": w["L0_gnn_W"], "gWT0": w["L0_gnn_W"].T, "gb0": w["L0_gnn_b"].reshape(1, P), "ga0": w["L0_gnn_a"],
        "gW1": w["L1_gnn_W"], "gWT1": w["L1_gnn_W"].T, "ga1": w["L1_gnn_a"].reshape(1, 2 * DH),
        "wgT": w["L0_ffn_Wg"].T, "bg": w["L0_ffn_bg"].reshape(1, E0),
        "w1T": w["L0_ffn_W1"].transpose(2, 0, 1),
        "b1": w["L0_ffn_b1"].reshape(E0, HC, P).transpose(2, 0, 1),
        "w2T": w["L0_ffn_W2"].reshape(E0, P, HC, P).transpose(3, 0, 2, 1), "b2": w["L0_ffn_b2"],
        "route": w["L1_ffn_route_id"].reshape(1, N // GRP),
        "wiT": w["L1_ffn_Wi"].T, "bi": w["L1_ffn_bi"].reshape(KC, P).T,
        "wrT": w["L1_ffn_Wr"].reshape(L, E1, HID, KC, P).transpose(4, 0, 1, 3, 2).reshape(P, L, E1, KC * HID),
        "br": w["L1_ffn_br"].transpose(1, 0, 2),
        "wsT": w["L1_ffn_Ws"].reshape(L, HID, KC, P).transpose(3, 0, 2, 1).reshape(P, L, KC * HID),
        "bs": w["L1_ffn_bs"].reshape(1, L, HID),
        "woT": w["L1_ffn_Wo"].reshape(P, KC, P).transpose(2, 1, 0), "bo": w["L1_ffn_bo"].reshape(1, P),
    }
    nc = bacc.Bacc("TRN2", target_bir_lowering=False, num_devices=1)
    arrays, args = {}, {}
    for name, v in lay.items():
        v = np.ascontiguousarray(v)
        arrays[f"in_{name}"] = v
        args[name] = nc.dram_tensor(f"in_{name}", v.shape, mybir.dt.from_np(v.dtype), kind="ExternalInput").ap()
    out = nc.dram_tensor("out_x", (N, P), F32, kind="ExternalOutput").ap()
    gnn_moe_stack(nc, args, out)
    r = run_bass_kernel_spmd(nc, [arrays], core_ids=[0])
    return r.results[0]["out_x"]
```

```python
from contextlib import ExitStack

import numpy as np

import concourse.bass as bass
from concourse import mybir

ALU = mybir.AluOpType
ACT = mybir.ActivationFunctionType
F32 = mybir.dt.float32
BF16 = mybir.dt.bfloat16
I32 = mybir.dt.int32
AX_X = mybir.AxisListType.X
RMAX = bass.bass_isa.ReduceOp.max

P = 128
N = 2048
T = N // P
CT = 4
C = T // CT
CW = CT * P
H = 4
DH = P // H
V1 = DH + 1
PARTS = 3
VW = PARTS * V1
QT = 4
Q = T // QT
E0 = 8
HC = 4
E1 = 16
HID = 256
KC = HID // P
L = 2
GRP = 32
GT = P // GRP
EPS = 1e-5
SLOPE = 0.2
SHIFT = 60.0
NEG = -3.0e38
XC = P + 2 * H


class Count:

    def __init__(self):
        self.n, self.off, self.bank = {}, {}, {}

    def event(self, name, by=1):
        self.n[name] = self.n.get(name, 0) + by
        return self.at(name)

    def at(self, name):
        return self.off.get(name, 0) + self.n.get(name, 0)

    def fill(self, b, name):
        self.event(name)
        self.bank[b] = (name, self.n[name])

    def freed(self, b):
        name, n = self.bank[b]
        return name, self.off.get(name, 0) + n

    def enter(self, i, first, per):
        self.at_entry = dict(self.n), dict(self.off), dict(self.bank)
        for name, by in per.items():
            self.off[name] = (i - first) * by + self.off.get(name, 0)

    def leave(self, turns, per):
        n0, off0, bank0 = self.at_entry
        made = {name: n - n0.get(name, 0) for name, n in self.n.items() if n != n0.get(name, 0)}
        assert made == per, (made, per)
        for b, (name, n) in self.bank.items():
            assert bank0.get(b) in ((name, n), (name, n - per.get(name, 0))), (b, name)
        for name, by in per.items():
            self.off[name] = (turns - 1) * by + off0.get(name, 0)


def gnn_moe_stack(nc, a, out):
    with ExitStack() as ctx:
        def sb(name, shape, dt=F32):
            return ctx.enter_context(nc.sbuf_tensor(name, shape, dt))

        def sem(name):
            return ctx.enter_context(nc.semaphore(name))

        maskT = sb("maskT", [P, T, N], BF16)
        x = sb("x", [P, T, P])
        hT = sb("hT", [P, N])
        hTc = sb("hTc", [P, CW])
        xc = sb("xc", [P, CT, P])
        xn = sb("xn", [P, CT, P])
        sbc = sb("sbc", [P, H, CW])
        odiv = xc
        att = sb("att", [P, CT * 2 * VW])
        ysb = sb("ysb", [P, 3, CW])
        arena = sb("arena", [P, 12288])
        wnat = [arena[:, s * P:(s + 1) * P] for s in range(2)]
        brep = arena[:, 2 * P:3 * P]
        ind = arena[:, 0:8192].bitcast(BF16).rearrange("p (q b j i) -> p q b j i", q=Q, b=2, j=QT)
        uf = arena[:, 3 * P:3 * P + T * H * 2 * V1].rearrange("p (g v) -> p g v", v=V1)
        whx0 = arena[:, 8192:8192 + T * XC].rearrange("p (t k) -> p t k", t=T)
        w1 = arena[:, 8192:10240].rearrange("p (s e f) -> p s e f", s=2, e=2)
        w2 = arena[:, 10240:12288].rearrange("p (s e c d) -> p s e c d", s=2, e=2, c=HC)
        whx1 = arena[:, 0:T * XC].rearrange("p (t k) -> p t k", t=T)
        wsel = arena[:, 0:8192].rearrange("p (s k n) -> p s k n", s=2 * L * GT, k=KC)
        at = [8192]

        def in_arena(parts, *dims):
            n = int(np.prod(dims))
            at[0] += n
            return arena[0:parts, at[0] - n:at[0]]

        wiT = in_arena(P, HID)
        bi = in_arena(P, KC)
        ws = in_arena(P, L, KC * HID).rearrange("p (l n) -> p l n", l=L)
        brs = in_arena(E1, L, HID).rearrange("p (l n) -> p l n", l=L)
        bsr = in_arena(E1, L, HID).rearrange("p (l n) -> p l n", l=L)
        woT = in_arena(P, KC, P).rearrange("p (k n) -> p k n", k=KC)
        bo = in_arena(1, P)
        tiles1 = sbc[:, :, :].rearrange("p h i -> p (h i)")
        htt = tiles1[:, 0:6 * HID].rearrange("p (r l n) -> p r l n", r=2, l=L + 1)
        hn = tiles1[:, 6 * HID:8 * HID].rearrange("p (r n) -> p r n", r=2)
        reg_b = sb("reg_b", [P, T * H * 2 * VW // 2])
        u = reg_b[:, :].bitcast(BF16).rearrange("p (g s v) -> p g s v", s=PARTS, v=V1)
        v1 = reg_b[:, 0:T * (P + 1)].rearrange("p (t v) -> p t v", t=T)
        rows1 = reg_b[:, T * (P + 1):T * (P + 1) + 2 * H * CW]
        reg_c = sb("reg_c", [P, 4096])
        adj = reg_c[:, :].bitcast(BF16).rearrange("p (s j) -> p s j", s=4)
        hid = reg_c[:, :].rearrange("p (e c i) -> p e c i", e=2, c=HC)
        prob = reg_c[:, :].rearrange("p (s i) -> p s i", s=8)
        wxs = [sb(f"wx{s}", [P, XC]) for s in range(2)]
        asel = [sb(f"asel{s}", [P, 2 * H]) for s in range(2)]
        wrep = sb("wrep", [P, H, P])
        ident = sb("ident", [P, P])
        identb = sb("identb", [P, P], BF16)
        ones = sb("ones", [P, P])
        consts = sb("consts", [P, 5])
        bcol = sb("bcol", [P, 1])
        bx = sb("bx", [1, XC])
        bac = sb("bac", [P, 2 * H])
        nmean = sb("nmean", [P, CT])
        svar = sb("svar", [P, CT])
        sstd = sb("sstd", [P, CT])
        rstd = sb("rstd", [P, CT])
        nd = sb("nd", [P, T, H])
        dsh = sb("dsh", [P, T, H])
        dsum = sb("dsum", [P, T])
        bd = sb("bd", [P, T, H, 2])
        ab = sb("ab", [P, T, H, 2])
        arg = sb("arg", [P, T, H, 2])
        zt = sb("zt", [P, T, H])
        zm = sb("zm", [P, T, H])
        pmax = sb("pmax", [P, 5])
        gmax = sb("gmax", [P, 2, 5])
        nmx = sb("nmx", [P, 5])
        red = sb("red", [P, 2 * CT, V1])
        wred = sb("wred", [P, 2 * CT, V1])
        num = sb("num", [P, CT, V1])
        rden = sb("rden", [P, CT])
        wgT = sb("wgT", [P, E0])
        bg = sb("bg", [1, E0])
        b1 = sb("b1", [P, E0, HC])
        b2 = sb("b2", [E0, P])
        sc = sb("sc", [P, CT, E0])
        sc2 = sb("sc2", [P, CT, E0])
        first_i = sb("first_i", [P, E0], I32)
        first_w = sb("first_w", [P, E0])
        oh = sb("oh", [P, 2, CT, E0])
        key = sb("key", [P, CT, E0])
        gst = sb("gst", [P, 8, CT])
        comb = sb("comb", [P, CT, E0])
        ohx = sb("ohx", [E1, CW])
        combT = ohx[0:E0, :].rearrange("e (t i) -> e t i", t=CT)
        route = sb("route", [1, N // GRP], I32)
        route16 = sb("route16", [E1, N // GRP], I32)
        routef = sb("routef", [E1, N // GRP])
        chan_i = sb("chan_i", [E1, 1], I32)
        chan = sb("chan", [E1, 1])
        onehot = sb("onehot", [E1, N // GRP])

        bank = [ctx.enter_context(nc.psum_tensor(f"bank{b}", [P, 512], F32)) for b in range(8)]
        bankb = [t[:, :].bitcast(BF16) for t in bank]

        full = [sem(f"bank{b}_full") for b in range(8)]
        s_x = [sem(f"x_chunk{c}_loaded") for c in range(C)]
        s_w = sem("small_weights_loaded")
        s_wp = [sem(f"expert_pair_slot{r}_loaded") for r in range(2)]
        s_w1 = sem("second_mixture_loaded")
        s_adj = [sem(f"adj_slot{r}_loaded") for r in range(4)]
        s_sel = [sem(f"selected_weights_slot{r}_loaded") for r in range(2 * L * GT)]
        s_const = sem("constants_ready")
        s_pool = sem("gpsimd_step_done")
        s_dve = sem("vector_step_done")
        s_brep = sem("bias_replicated")
        s_rep = sem("replicated_score_weights_ready")
        s_var = sem("chunk_variance_ready")
        s_std = sem("chunk_deviation_ready")
        s_xn = sem("chunk_normalised")
        s_pm = sem("partition_maxima_ready")
        s_gm = sem("global_maxima_ready")
        s_arg = sem("exponents_ready")
        s_exp = sem("exponentials_ready")
        s_u = sem("values_ready")
        s_g = sem("indicator_above_ready")
        s_ind = sem("indicator_quad_ready")
        s_indf = sem("indicator_quad_used")
        s_attf = sem("attention_sums_used")
        s_gap = sem("gate_gap_ready")
        s_gex = sem("gate_exp_ready")
        s_comb = sem("combine_weights_ready")
        s_acc = sem("weighted_output_added")
        s_step = sem("product_step_done")
        s_prob = sem("probability_tile_ready")
        s_probf = sem("probability_quad_used")
        s_wc = sem("shared_weights_summed")
        s_ohx = sem("onehot_chunk_ready")
        s_out = sem("output_stored")
        ev = {name: sem(what) for name, what in (
            ("ext", "score_weights_ready"), ("mask", "mask_half_row_ready"), ("hTc", "chunk_transposed"),
            ("proj", "projected_half_chunk_ready"), ("rows", "source_row_ready"), ("att", "attention_sums_ready"),
            ("sc", "gate_scores_ready"), ("combT", "combine_weights_transposed"), ("hid", "hidden_block_ready"),
            ("y", "weighted_output_ready"), ("htt", "hidden_tile_ready"))}
        NW = 4 + 2 * H + 8
        NW1 = 7
        NC = 8
        BANK3 = 2 * C + C * E0 * HC // 2
        BANK5 = C * (E0 // 2 + 1)
        FFN_Y = C * (E0 + 1)
        block = ctx.enter_context(nc.Block())

        def more(ap, n):
            return ap.unsqueeze(len(ap.shape)).to_broadcast([*ap.shape, n])

        @block.sync
        def _(sp):
            xin = a["x"].rearrange("(t p) d -> p t d", p=P)
            for c in range(C):
                sp.dma_start(x[:, c * CT:(c + 1) * CT, :], xin[:, c * CT:(c + 1) * CT, :]).then_inc(s_x[c], 16)
            sp.wait_ge(s_const, NC)
            with nc.allow_non_contiguous_dma(reason="small vectors"):
                for s in range(2):
                    sp.dma_start(wnat[s], a[f"gW{s}"]).then_inc(s_w, 16)
                    sp.dma_start(wxs[s][:, 0:P], a[f"gWT{s}"]).then_inc(s_w, 16)
                for h in range(H):
                    for s in range(2):
                        src = a["ga0"][h:h + 1, :] if s == 0 else a["ga1"]
                        sp.dma_start(asel[s][h * DH:(h + 1) * DH, h:2 * H:H],
                                     src.rearrange("o (k d) -> (o d) k", k=2)).then_inc(s_w, 16)
                sp.dma_start(bcol[:, :], a["gb0"].rearrange("o k -> k o")).then_inc(s_w, 16)
            sp.dma_start(bx[0:1, 0:P], a["gb0"]).then_inc(s_w, 16)
            sp.dma_start(wgT[:, :], a["wgT"]).then_inc(s_w, 16)
            sp.dma_start(bg[:, :], a["bg"]).then_inc(s_w, 16)
            sp.dma_start(b1[:, :, :], a["b1"]).then_inc(s_w, 16)
            sp.dma_start(b2[:, :], a["b2"]).then_inc(s_w, 16)
            sp.dma_start(route[:, :], a["route"]).then_inc(s_w, 16)
            sp.dma_start(route16[:, :], a["route"].to_broadcast([E1, N // GRP])).then_inc(s_w, 16)
            sp.wait_ge(s_u, 1)

            def load_pair(c, h, wait):
                if wait:
                    sp.wait_ge(full[5], c * (H + 1) + (h if h >= 2 else h - 1))
                e = slice(2 * h, 2 * h + 2)
                sp.dma_start(w1[:, h % 2, :, :], a["w1T"][:, e, :]).then_inc(s_wp[h % 2], 16)
                sp.dma_start(w2[:, h % 2, :, :, :], a["w2T"][:, e, :, :]).then_inc(s_wp[h % 2], 16)

            for h in range(H):
                load_pair(0, h, h >= 2)
            with sp.Fori(1, C) as c:
                for h in range(H):
                    load_pair(c, h, True)
            sp.wait_ge(s_acc, FFN_Y)
            sp.dma_start(wiT, a["wiT"]).then_inc(s_w1, 16)
            sp.dma_start(bi, a["bi"]).then_inc(s_w1, 16)
            sp.dma_start(ws, a["wsT"]).then_inc(s_w1, 16)
            sp.dma_start(brs, a["br"]).then_inc(s_w1, 16)
            sp.dma_start(bsr, a["bs"].to_broadcast([E1, L, HID])).then_inc(s_w1, 16)
            sp.dma_start(woT, a["woT"]).then_inc(s_w1, 16)
            sp.dma_start(bo, a["bo"]).then_inc(s_w1, 16)

            def select(pair, wait):
                for r in range(2):
                    for l in range(L):
                        for g in range(GT):
                            s = (r * L + l) * GT + g
                            e = sp.value_load(route[0:1, bass.ds(pair * 2 * GT + r * GT + g, 1)], min_val=0,
                                              max_val=E1 - 1)
                            if wait:
                                sp.wait_ge(full[3 + 2 * r],
                                           (pair - 1) * (L + 1) + ((BANK5 if r else BANK3) + l + 1))
                            sp.dma_start(wsel[:, s, :, :].rearrange("p k n -> p (k n)").unsqueeze(1),
                                         a["wrT"][:, l, bass.ds(e, 1), :]).then_inc(s_sel[s], 16)

            sp.wait_ge(s_u, 2)
            sp.wait_ge(s_exp, 3)
            select(0, False)
            with sp.Fori(1, T // 2) as pair:
                select(pair, True)

        @block.gpsimd
        def _(pool):
            nc.gpsimd.memset(ident[:, :], 0.0).then_inc(s_pool, 1)
            for m in (asel[0], asel[1]):
                nc.gpsimd.memset(m[:, :], 0.0).then_inc(s_const, 1)
            nc.gpsimd.memset(ones[:, :], 1.0).then_inc(s_const, 1)
            for i, v in enumerate((EPS, SHIFT, SLOPE * SHIFT, -SHIFT, -SLOPE * SHIFT)):
                last = nc.gpsimd.memset(consts[:, i:i + 1], v)
            last.then_inc(s_const, 1)
            nc.gpsimd.iota(first_i[:, :], pattern=[[-1, E0]], base=E0, channel_multiplier=0).then_inc(s_pool, 1)
            nc.gpsimd.iota(chan_i[:, :], pattern=[[0, 1]], base=0, channel_multiplier=1).then_inc(s_pool, 1)
            pool.wait_ge(s_pool, 3)
            nc.gpsimd.affine_select(out=ident[:, :], in_=ident[:, :], compare_op=ALU.not_equal, fill=1.0,
                                    base=0, pattern=[[-1, P]], channel_multiplier=1).then_inc(s_pool, 1)
            nc.gpsimd.tensor_copy(first_w[:, :], first_i[:, :]).then_inc(s_const, 1)
            nc.gpsimd.tensor_copy(chan[:, :], chan_i[:, :]).then_inc(s_const, 1)
            pool.wait_ge(s_pool, 4)
            nc.gpsimd.tensor_copy(identb[:, :], ident[:, :]).then_inc(s_const, 1)
            nc.gpsimd.memset(pmax[:, :], 0.0).then_inc(s_const, 1)

            def load_rows(r):
                if r >= 4:
                    pool.wait_ge(full[7], r - 3 + (2 if r >= 8 else 0))
                pool.dma_start(adj[:, r % 4, :], a["adj"][r * P:(r + 1) * P, :]).then_inc(s_adj[r % 4], 16)

            for r in range(8):
                load_rows(r)
            pool.wait_ge(s_pm, 1)
            nc.gpsimd.partition_all_reduce(gmax[:, 0, :], pmax[:, :], P, RMAX).then_inc(s_gm, 1)
            for r in range(8, T):
                load_rows(r)

            for n in range(FFN_Y):
                c, e = divmod(n, E0 + 1)
                pool.wait_ge(ev["y"], n + 1)
                if e:
                    pool.wait_ge(s_acc, n)
                xi = x[:, c * CT:(c + 1) * CT, :]
                nc.gpsimd.tensor_tensor(xi, xi, ysb[:, e % 3, :].rearrange("p (t d) -> p t d", d=P),
                                        ALU.add).then_inc(s_acc, 1)
            pool.wait_ge(s_w, 16 * NW)
            nc.gpsimd.tensor_copy(routef[:, :], route16[:, :]).then_inc(s_pool, 1)
            pool.wait_ge(s_pool, 5)
            nc.gpsimd.tensor_scalar(onehot[:, :], routef[:, :], chan[:, 0:1], None,
                                    ALU.is_equal).then_inc(s_pool, 1)
            pool.wait_ge(s_w1, 16 * NW1)
            nc.gpsimd.tensor_tensor(brs, brs, bsr, ALU.add).then_inc(s_wc, 1)
            for l in range(L):
                for kc in range(KC):
                    d = ws[:, l, kc * HID + kc * P:kc * HID + (kc + 1) * P]
                    nc.gpsimd.tensor_tensor(d, d, ident[:, :], ALU.add).then_inc(s_wc, 1)
            pool.wait_ge(s_pm, 2)
            nc.gpsimd.partition_all_reduce(gmax[:, 1, :], pmax[:, :], P, RMAX).then_inc(s_gm, 1)
            pool.wait_ge(s_pool, 6)
            outv = out.rearrange("(t p) d -> p t d", p=P)
            for c in range(C):
                nc.gpsimd.tensor_copy(ohx[:, :].rearrange("e (g i) -> e g i", i=GRP),
                                      more(onehot[:, c * CT * GT:(c + 1) * CT * GT], GRP)).then_inc(s_ohx, 1)
                for i in range(CT):
                    pool.wait_ge(ev["y"], FFN_Y + c * CT + i + 1)
                    xi = x[:, c * CT + i, :]
                    nc.gpsimd.tensor_tensor(xi, xi, ysb[:, 0, i * P:(i + 1) * P], ALU.add).then_inc(s_acc, 1)
                pool.wait_ge(s_acc, FFN_Y + c * CT + CT)
                pool.dma_start(outv[:, c * CT:(c + 1) * CT, :],
                               x[:, c * CT:(c + 1) * CT, :]).then_inc(s_out, 16)
            pool.wait_ge(s_out, 16 * C)

        @block.tensor
        def _(pe):
            k = Count()
            mm = nc.tensor.matmul

            def use(b, event):
                if b in k.bank:
                    name, v = k.freed(b)
                    pe.wait_ge(ev[name], v)
                k.fill(b, event)

            def ln_transpose():
                pe.wait_ge(s_xn, k.event("xn"))
                use(6, "hTc")
                for i in range(CT):
                    last = nc.tensor.transpose(bank[6][:, i * P:(i + 1) * P], xn[:, i, :], ident[:, :])
                last.then_inc(full[6], 1)
                pe.wait_ge(ev["hTc"], k.at("hTc"))

            def mask_rows(r):
                pe.wait_ge(s_adj[r % 4], 16 * (r // 4 + 1))
                for half in range(2):
                    b = 6 + half
                    use(b, "mask")
                    for j in range(T // 2):
                        jt = half * T // 2 + j
                        last = nc.tensor.transpose(bankb[b][:, j * P:(j + 1) * P],
                                                   adj[:, r % 4, jt * P:(jt + 1) * P], identb[:, :])
                    last.then_inc(full[b], 1)

            def project(s):
                for i in range(CT):
                    b = 2 + i // 2
                    if i % 2 == 0:
                        use(b, "proj")
                    o = bank[b][:, (i % 2) * XC:(i % 2 + 1) * XC]
                    last = mm(o, hTc[:, i * P:(i + 1) * P], wxs[s][:, :], start=True, stop=(s == 1))
                    if s == 0:
                        last = mm(o, ones[0:1, :], bx[:, :], start=False, stop=True)
                    if i % 2:
                        last.then_inc(full[b], 1)

            def source_rows(s, c):
                for h in range(H):
                    b = 6 + h % 2
                    use(b, "rows")
                    mm(bank[b][:, :], wrep[:, h, :], hT[:, bass.ts(c, CW)], start=True,
                       stop=True).then_inc(full[b], 1)

            def attend(h):
                use(0, "att")
                use(1, "att")
                for q in range(Q):
                    pe.wait_ge(s_ind, k.event("ind"))
                    for j in range(QT):
                        t = q * QT + j
                        for i in range(CT):
                            for b in range(2):
                                o = (i % 2) * 2 * VW + b * VW
                                last = mm(bank[i // 2][:, o:o + VW], ind[:, q, b, j, i * P:(i + 1) * P],
                                          u[:, (t * H + h) * 2 + b, :, :],
                                          start=(t == 0 and i % 2 == 0 and b == 0), stop=(t == T - 1),
                                          skip_group_check=True)
                            if t == T - 1 and i % 2:
                                last.then_inc(full[i // 2], 1)
                    if q < Q - 1:
                        last.then_inc(s_indf, 1)

            def gate():
                ln_transpose()
                use(4, "sc")
                for i in range(CT):
                    o = bank[4][:, i * E0:(i + 1) * E0]
                    mm(o, hTc[:, i * P:(i + 1) * P], wgT[:, :], start=True, stop=False)
                    last = mm(o, ones[0:1, :], bg[:, :], start=False, stop=True)
                last.then_inc(full[4], 1)
                pe.wait_ge(s_comb, k.event("comb"))
                use(6, "combT")
                for i in range(CT):
                    last = nc.tensor.transpose(bank[6][0:E0, i * P:(i + 1) * P], comb[:, i, :], ident[:, :])
                last.then_inc(full[6], 1)
                pe.wait_ge(ev["combT"], k.at("combT"))
                use(5, "y")
                for i in range(CT):
                    last = mm(bank[5][:, i * P:(i + 1) * P], combT[:, i, :], b2[:, :], start=True, stop=True)
                last.then_inc(full[5], 1)

            def experts(pair):
                s = pair % 2
                pe.wait_ge(s_wp[s], k.event(f"pair{s}", 32))
                for e in (2 * pair, 2 * pair + 1):
                    for c in range(HC):
                        b = 2 + c % 2
                        use(b, "hid")
                        mm(bank[b][:, :], w1[:, s, e % 2, c * P:(c + 1) * P], hTc[:, :], start=True,
                           stop=True).then_inc(full[b], 1)
                for e in (2 * pair, 2 * pair + 1):
                    b = 4 + e % 2
                    use(b, "y")
                    pe.wait_ge(ev["hid"], k.at("hid") - (HC if e % 2 == 0 else 0))
                    for i in range(CT):
                        for c in range(HC):
                            last = mm(bank[b][:, i * P:(i + 1) * P], hid[:, e % 2, c, i * P:(i + 1) * P],
                                      w2[:, s, e % 2, c, :], start=(c == 0), stop=(c == HC - 1))
                    last.then_inc(full[b], 1)

            pe.wait_ge(s_w, 16 * NW)
            pe.wait_ge(s_const, NC)
            pe.wait_ge(s_brep, 1)
            use(6, "ext")
            mm(bank[6][:, 0:8], wnat[0], asel[0][:, :], start=True, stop=True)
            mm(bank[6][:, 8:16], wnat[1], asel[1][:, :], start=True, stop=True)
            mm(bank[6][:, 16:24], brep, asel[0][:, :], start=True, stop=True)
            mm(bank[6][0:1, 24:32], bcol[:, :], asel[0][:, :], start=True, stop=True).then_inc(full[6], 1)
            for r in range(CT):
                mask_rows(r)
            per = {"xn": 1, "hTc": 1, "proj": 2}
            ln_transpose()
            project(0)
            with pe.Fori(1, C) as c:
                k.enter(c, 1, per)
                ln_transpose()
                project(0)
                k.leave(C - 1, per)
            pe.wait_ge(s_rep, H)
            source_rows(0, 0)
            pe.wait_ge(s_u, 1)
            for h in range(H):
                attend(h)
                for r in range(CT + 3 * h, CT + 3 * h + 3):
                    mask_rows(r)
            source_rows(0, 1)

            def chunk0(c, next_rows):
                for h in range(H):
                    attend(h)
                    if h == H - 1:
                        source_rows(0, next_rows)
                    if h == 0:
                        gate()
                    experts(h)

            chunk0(1, 2)
            per = {"att": 8, "ind": 16, "rows": 4, "xn": 1, "hTc": 1, "sc": 1, "comb": 1, "combT": 1,
                   "hid": 32, "y": 9, "pair0": 64, "pair1": 64}
            with pe.Fori(2, C) as c:
                k.enter(c, 2, per)
                chunk0(c, (c + 1) % C)
                k.leave(C - 2, per)
            gate()
            for h in range(H):
                experts(h)

            per = {"xn": 1, "hTc": 1, "proj": 2}
            ln_transpose()
            project(1)
            with pe.Fori(1, C) as c:
                k.enter(c, 1, per)
                ln_transpose()
                project(1)
                k.leave(C - 1, per)
            pe.wait_ge(s_rep, 2 * H)
            source_rows(1, 0)
            pe.wait_ge(s_u, 2)

            def attend1(t):
                if t == 0:
                    use(0, "att")
                    use(1, "att")
                pe.wait_ge(s_prob, k.event("prob"))
                for i in range(CT):
                    b, o = (0, i * (P + 1)) if i < 3 else (1, 0)
                    last = mm(bank[b][:, o:o + P + 1], prob[:, t % 8, i * P:(i + 1) * P], v1[:, t, :],
                              start=(t == 0 and i in (0, 3)), stop=(t == T - 1), skip_group_check=True)
                    if t == T - 1 and i >= 2:
                        last.then_inc(full[b], 1)
                if t % QT == QT - 1 and t < T - 1:
                    last.then_inc(s_probf, 1)

            def ready(b):
                name, v = k.freed(b)
                pe.wait_ge(ev[name], v)

            def hidden(i):
                b = 2 + i % 2 * 2
                use(b, "htt")
                for m in range(KC):
                    last = mm(bank[b][:, m * P:(m + 1) * P], wiT[:, m * P:(m + 1) * P],
                              hTc[:, i * P:(i + 1) * P], start=True, stop=True)
                last.then_inc(full[b], 1)

            def layer(i, l):
                r, b = i % 2, 3 + i % 2 * 2
                o = bank[b][:, 0:HID]
                use(b, "htt")
                mm(o, ohx[:, i * P:(i + 1) * P], brs[:, l, :], start=True, stop=False, skip_group_check=True)
                ready(b - 1)
                for kc in range(KC):
                    mm(o, htt[:, r, l, kc * P:(kc + 1) * P], ws[:, l, kc * HID:(kc + 1) * HID],
                       start=False, stop=False, skip_group_check=True)
                for g in range(GT):
                    s = (r * L + l) * GT + g
                    pe.wait_ge(s_sel[s], k.event(f"sel{r}{l}{g}", 16))
                    for kc in range(KC):
                        c = kc * P + g * GRP
                        last = mm(bank[b][g * GRP:(g + 1) * GRP, 0:HID], htt[:, r, l, c:c + GRP],
                                  wsel[:, s, kc, :], start=False, stop=(kc == KC - 1),
                                  skip_group_check=True, tile_position=(0, g * GRP))
                last.then_inc(full[b], 1)

            def turn(i):
                b = 2 + i % 2 * 2
                ready(b + 1)
                use(b, "htt")
                for kc in range(KC):
                    last = nc.tensor.transpose(bank[b][:, kc * P:(kc + 1) * P],
                                               hn[:, i % 2, kc * P:(kc + 1) * P], ident[:, :])
                last.then_inc(full[b], 1)

            def output(i):
                r, b = i % 2, 3 + i % 2 * 2
                ready(b - 1)
                use(b, "y")
                for kc in range(KC):
                    mm(bank[b][:, 0:P], htt[:, r, L, kc * P:(kc + 1) * P], woT[:, kc, :], start=(kc == 0),
                       stop=False)
                mm(bank[b][:, 0:P], ones[0:1, :], bo[:, :], start=False, stop=True).then_inc(full[b], 1)

            for t in range(T):
                attend1(t)
                if t == QT - 1:
                    source_rows(1, 1)
            pe.wait_ge(s_wc, 1 + L * KC)

            def chunk1(next_rows):
                for t in range(QT):
                    attend1(t)
                source_rows(1, next_rows)
                ln_transpose()
                pe.wait_ge(s_ohx, k.event("ohx"))
                hidden(0)
                for i in range(CT):
                    for l in range(L):
                        layer(i, l)
                        attend1(QT + 3 * i + 2 * l)
                        turn(i)
                        if l == 0:
                            attend1(QT + 3 * i + 1)
                    if i < CT - 1:
                        hidden(i + 1)
                    output(i)

            chunk1(2)
            per = {"att": 2, "prob": 16, "rows": 4, "xn": 1, "hTc": 1, "ohx": 1, "htt": 20, "y": 4}
            per.update({f"sel{r}{l}{g}": 32 for r in range(2) for l in range(L) for g in range(GT)})
            with pe.Fori(2, C) as c:
                k.enter(c, 2, per)
                chunk1((c + 1) % C)
                k.leave(C - 2, per)
            ln_transpose()
            pe.wait_ge(s_ohx, k.event("ohx"))
            for i in range(0, CT, 2):
                pair = (i, i + 1)
                for j in pair:
                    hidden(j)
                for l in range(L):
                    for j in pair:
                        layer(j, l)
                    for j in pair:
                        turn(j)
                for j in pair:
                    output(j)

        @block.scalar
        def _(act):
            k = Count()
            af = nc.scalar.activation

            def got(b):
                act.wait_ge(full[b], k.event(f"full{b}"))

            def ln_std():
                act.wait_ge(s_var, k.event("var"))
                af(sstd[:, :], svar[:, :], ACT.Sqrt, bias=consts[:, 0:1], scale=1.0 / P).then_inc(s_std, 1)

            def ln_out(c=None):
                got(6)
                if c is not None:
                    af(hT[:, bass.ts(c, CW)], bank[6][:, :], ACT.Copy)
                af(hTc[:, :], bank[6][:, :], ACT.Copy).then_inc(ev["hTc"], 1)

            def mask_rows(r):
                for half in range(2):
                    b = 6 + half
                    got(b)
                    af(maskT[:, half * 8:(half + 1) * 8, r * P:(r + 1) * P],
                       bankb[b].rearrange("p (j i) -> p j i", i=P), ACT.Copy).then_inc(ev["mask"], 1)

            def project(whx, c):
                for half in range(2):
                    b = 2 + half
                    got(b)
                    af(whx[:, bass.ds(c * CT + 2 * half, 2), :],
                       bank[b][:, 0:2 * XC].rearrange("p (t k) -> p t k", t=2), ACT.Copy).then_inc(ev["proj"], 1)

            def source_rows(s, parity=0):
                for h in range(H):
                    b = 6 + h % 2
                    got(b)
                    if s == 0:
                        af(sbc[:, h, :], bank[b][:, :], ACT.Copy).then_inc(ev["rows"], 1)
                    else:
                        af(rows1[:, bass.ds((parity * H + h) * CW, CW)], bank[b][:, :], ACT.Exp, bias=nmx[:, h:h + 1],
                           scale=SLOPE).then_inc(ev["rows"], 1)

            def sums(*widths):
                v = k.event("sums") - 1
                if not (isinstance(v, int) and v <= 0):
                    act.wait_ge(s_attf, v)
                o = 0
                for b, w in enumerate(widths):
                    got(b)
                    af(att[:, o:o + w], bank[b][:, 0:w], ACT.Copy).then_inc(ev["att"], 1)
                    o += w

            def y_slot(slots):
                v = k.event("y") - slots
                if not (isinstance(v, int) and v <= 0):
                    act.wait_ge(s_acc, v)

            def gate():
                ln_std()
                ln_out()
                got(4)
                af(sc[:, :, :], bank[4][:, 0:CT * E0].rearrange("p (t e) -> p t e", e=E0),
                   ACT.Copy).then_inc(ev["sc"], 1)
                act.wait_ge(s_gap, k.event("gap"))
                af(gst[:, 3, :], gst[:, 2, :], ACT.Exp).then_inc(s_gex, 1)
                got(6)
                af(combT[:, :, :], bank[6][0:E0, :].rearrange("p (t i) -> p t i", i=P),
                   ACT.Copy).then_inc(ev["combT"], 1)
                y_slot(3)
                got(5)
                af(ysb[:, 0, :], bank[5][:, :], ACT.Copy).then_inc(ev["y"], 1)

            def experts(pair):
                for e in (2 * pair, 2 * pair + 1):
                    for c in range(HC):
                        got(2 + c % 2)
                        af(hid[:, e % 2, c, :], bank[2 + c % 2][:, :], ACT.Relu,
                           bias=b1[:, e, c:c + 1]).then_inc(ev["hid"], 1)
                for e in (2 * pair, 2 * pair + 1):
                    y_slot(3)
                    got(4 + e % 2)
                    for i in range(CT):
                        last = af(ysb[:, (e + 1) % 3, i * P:(i + 1) * P],
                                  bank[4 + e % 2][:, i * P:(i + 1) * P], ACT.Copy, scale=comb[:, i, e:e + 1])
                    last.then_inc(ev["y"], 1)

            got(6)
            af(wxs[0][:, P:XC], bank[6][:, 0:8], ACT.Copy)
            af(wxs[1][:, P:XC], bank[6][:, 8:16], ACT.Copy)
            af(bac[:, :], bank[6][:, 16:24], ACT.Copy)
            af(bx[0:1, P:XC], bank[6][0:1, 24:32], ACT.Copy).then_inc(ev["ext"], 1)
            for r in range(CT):
                mask_rows(r)

            def prelude(whx):
                per = {"var": 1, "full6": 1, "full2": 1, "full3": 1}
                with act.Fori(0, C) as c:
                    k.enter(c, 0, per)
                    ln_std()
                    ln_out(c)
                    project(whx, c)
                    k.leave(C, per)

            prelude(whx0)
            act.wait_ge(s_arg, 1)
            af(bd[:, :, :, 0], dsh[:, :, :], ACT.Exp, bias=consts[:, 1:2])
            af(bd[:, :, :, 1], dsh[:, :, :], ACT.Exp, bias=consts[:, 2:3], scale=SLOPE).then_inc(s_exp, 1)
            act.wait_ge(s_arg, 2)
            af(ab[:, :, :, 0], arg[:, :, :, 0], ACT.Exp, bias=consts[:, 3:4])
            af(ab[:, :, :, 1], arg[:, :, :, 1], ACT.Exp, bias=consts[:, 4:5]).then_inc(s_exp, 1)
            source_rows(0)
            for h in range(H):
                sums(4 * VW, 4 * VW)
                for r in range(CT + 3 * h, CT + 3 * h + 3):
                    mask_rows(r)
            source_rows(0)
            per = {"sums": 4, "full0": 4, "full1": 4, "full6": 4, "full7": 2, "var": 1, "full4": 5, "gap": 1,
                   "full5": 5, "y": 9, "full2": 16, "full3": 16}

            def chunk0():
                for h in range(H):
                    sums(4 * VW, 4 * VW)
                    if h == H - 1:
                        source_rows(0)
                    if h == 0:
                        gate()
                    experts(h)

            chunk0()
            with act.Fori(2, C) as c:
                k.enter(c, 2, per)
                chunk0()
                k.leave(C - 2, per)
            gate()
            for h in range(H):
                experts(h)

            prelude(whx1)
            act.wait_ge(s_arg, 3)
            for h in range(H):
                af(nd[:, :, h], whx1[:, :, P + H + h], ACT.Exp, bias=nmx[:, h:h + 1], scale=-SLOPE)
            af(v1[:, :, P], dsum[:, :], ACT.Exp, bias=nmx[:, 4:5], scale=1.0 / H).then_inc(s_exp, 1)
            act.wait_ge(s_u, 2)
            source_rows(1, 0)
            source_rows(1, 1)
            sums(3 * (P + 1), P + 1)

            def hidden(i):
                b = 2 + i % 2 * 2
                got(b)
                for m in range(KC):
                    last = af(htt[:, i % 2, 0, m * P:(m + 1) * P], bank[b][:, m * P:(m + 1) * P], ACT.Relu,
                              bias=bi[:, m:m + 1])
                last.then_inc(ev["htt"], 1)

            def layer(i):
                b = 3 + i % 2 * 2
                got(b)
                af(hn[:, i % 2, :], bank[b][:, 0:HID], ACT.Relu).then_inc(ev["htt"], 1)

            def turn(i, l):
                b = 2 + i % 2 * 2
                got(b)
                af(htt[:, i % 2, l + 1, :], bank[b][:, 0:HID], ACT.Copy).then_inc(ev["htt"], 1)

            def output(i):
                b = 3 + i % 2 * 2
                y_slot(CT)
                got(b)
                af(ysb[:, 0, i * P:(i + 1) * P], bank[b][:, 0:P], ACT.Copy).then_inc(ev["y"], 1)

            per = {"sums": 1, "full0": 1, "full1": 1, "full6": 3, "full7": 2, "var": 1, "full2": 6, "full3": 6,
                   "full4": 6, "full5": 6, "y": 4}
            with act.Fori(1, C) as c:
                k.enter(c, 1, per)
                source_rows(1, (c + 1) % 2)
                ln_std()
                ln_out()
                hidden(0)
                for i in range(CT):
                    layer(i)
                    turn(i, 0)
                    layer(i)
                    if i == CT - 1:
                        sums(3 * (P + 1), P + 1)
                    turn(i, 1)
                    if i < CT - 1:
                        hidden(i + 1)
                    output(i)
                k.leave(C - 1, per)
            ln_std()
            ln_out()
            for i in range(0, CT, 2):
                pair = (i, i + 1)
                for j in pair:
                    hidden(j)
                for l in range(L):
                    for j in pair:
                        layer(j)
                    for j in pair:
                        turn(j, l)
                for j in pair:
                    output(j)

        @block.vector
        def _(dve):
            k = Count()
            v = nc.vector

            def then(ins):
                ins.then_inc(s_dve, 1)
                dve.wait_ge(s_dve, k.event("dve"))

            def norm(c, unit):
                xi = x[:, bass.ts(c, CT), :]
                then(v.tensor_scalar(xc[:, :, :], xi, -1.0 / P, None, ALU.mult))
                then(v.reduce_sum(nmean[:, :], xc[:, :, :], AX_X))
                then(v.tensor_tensor(xc[:, :, :], xi, more(nmean[:, :], P), ALU.add))
                if not (isinstance(unit, int) and unit == 0):
                    dve.wait_ge(ev["hTc"], unit)
                then(v.tensor_tensor(xn[:, :, :], xc[:, :, :], xc[:, :, :], ALU.mult))
                v.reduce_sum(svar[:, :], xn[:, :, :], AX_X).then_inc(s_var, 1)
                dve.wait_ge(s_std, unit + 1)
                then(v.reciprocal(rstd[:, :], sstd[:, :]))
                v.tensor_tensor(xn[:, :, :], xc[:, :, :], more(rstd[:, :], P), ALU.mult).then_inc(s_xn, 1)
                dve.wait_ge(s_xn, unit + 1)

            dve.wait_ge(s_const, NC)
            dve.wait_ge(s_w, 16 * NW)
            v.tensor_scalar(brep, ones[:, :], bcol[:, 0:1], None, ALU.mult).then_inc(s_brep, 1)
            dve.wait_ge(ev["ext"], 1)
            def replicate(s):
                for h in range(H):
                    v.tensor_scalar(wrep[:, h, :], ones[:, :], wxs[s][:, P + h:P + h + 1], None,
                                    ALU.mult).then_inc(s_rep, 1)

            replicate(0)
            for c in range(C):
                dve.wait_ge(s_x[c], 16)

            def norms(unit0):
                with dve.Fori(0, C) as c:
                    k.enter(c, 0, {"dve": 5})
                    norm(c, c + unit0)
                    k.leave(C, {"dve": 5})

            def norms_first():
                norm(0, 0)
                with dve.Fori(1, C) as c:
                    k.enter(c, 1, {"dve": 5})
                    norm(c, c)
                    k.leave(C - 1, {"dve": 5})

            norms_first()

            dve.wait_ge(ev["proj"], 2 * C)
            S0, D0 = whx0[:, :, P:P + H], whx0[:, :, P + H:P + 2 * H]
            v.scalar_tensor_tensor(nd[:, :, :], D0, -1.0,
                                   bac[:, 0:H].unsqueeze(1).to_broadcast([P, T, H]), ALU.mult, ALU.subtract)
            v.tensor_reduce(pmax[:, 0:H], D0.rearrange("p t h -> p h t"), AX_X, ALU.max).then_inc(s_pm, 1)
            dve.wait_ge(s_gm, 1)
            g0 = gmax[:, 0, 0:H].unsqueeze(1).to_broadcast([P, T, H])
            v.tensor_tensor(dsh[:, :, :], D0, g0, ALU.subtract).then_inc(s_arg, 1)
            then(v.tensor_tensor(zt[:, :, :], S0, g0, ALU.add))
            then(v.scalar_tensor_tensor(zm[:, :, :], zt[:, :, :], SLOPE, zt[:, :, :], ALU.mult, ALU.max))
            v.tensor_tensor(arg[:, :, :, 0], zt[:, :, :], zm[:, :, :], ALU.subtract)
            v.scalar_tensor_tensor(arg[:, :, :, 1], zt[:, :, :], SLOPE, zm[:, :, :], ALU.mult,
                                   ALU.subtract).then_inc(s_arg, 1)
            dve.wait_ge(s_exp, 1)
            uf4 = uf.rearrange("p (t h b) v -> p t h b v", t=T, h=H)
            for b in range(2):
                v.tensor_tensor(uf4[:, :, :, b, 0:DH], whx0[:, :, 0:P].rearrange("p t (h d) -> p t h d", h=H),
                                more(bd[:, :, :, b], DH), ALU.mult)
            then(v.tensor_copy(uf[:, :, DH], bd[:, :, :, :].rearrange("p t h b -> p (t h b)")))
            then(v.tensor_copy(u[:, :, 0, :], uf))
            then(v.tensor_tensor(uf, uf, u[:, :, 0, :], ALU.subtract))
            then(v.tensor_copy(u[:, :, 1, :], uf))
            v.tensor_tensor(u[:, :, 2, :], uf, u[:, :, 1, :], ALU.subtract).then_inc(s_u, 1)

            def indicate(c, h):
                n = c * H + h
                cs = bass.ts(c, CW)
                for q in range(Q):
                    if not (isinstance(n, int) and n == 0):
                        if q < Q - 1:
                            dve.wait_ge(s_indf, n * (Q - 1) + (q + 1 - (Q - 1)))
                        else:
                            dve.wait_ge(full[1], n)
                    for j in range(QT):
                        t = q * QT + j
                        last = v.scalar_tensor_tensor(ind[:, q, 0, j, :], sbc[:, h, :], nd[:, t, h:h + 1],
                                                      maskT[:, t, cs], ALU.is_gt, ALU.mult)
                    last.then_inc(s_g, 1)
                    dve.wait_ge(s_g, n * Q + (q + 1))
                    v.tensor_tensor(ind[:, q, 1, :, :], maskT[:, q * QT:(q + 1) * QT, cs], ind[:, q, 0, :, :],
                                    ALU.subtract).then_inc(s_ind, 1)

            def merge(c, h):
                n = c * H + h
                dve.wait_ge(ev["att"], n * 2 + 2)
                a4 = att[:, :].rearrange("p (g s v) -> p g s v", s=PARTS, v=V1)
                then(v.tensor_tensor(red[:, :, :], a4[:, :, 1, :], a4[:, :, 2, :], ALU.add))
                v.tensor_tensor(red[:, :, :], red[:, :, :], a4[:, :, 0, :], ALU.add).then_inc(s_attf, 1)
                dve.wait_ge(s_attf, n + 1)
                dve.wait_ge(s_exp, 2)
                then(v.tensor_tensor(wred[:, :, :].rearrange("p (t b) v -> p t b v", b=2),
                                     red[:, :, :].rearrange("p (t b) v -> p t b v", b=2),
                                     more(ab[:, bass.ts(c, CT), h, :], V1), ALU.mult))
                w4 = wred[:, :, :].rearrange("p (t b) v -> p t b v", b=2)
                then(v.tensor_tensor(num[:, :, :], w4[:, :, 0, :], w4[:, :, 1, :], ALU.add))
                then(v.reciprocal(rden[:, :], num[:, :, DH]))
                then(v.tensor_tensor(odiv[:, :, 0:DH], num[:, :, 0:DH], more(rden[:, :], DH), ALU.mult))
                xo = x[:, bass.ts(c, CT), h * DH:(h + 1) * DH]
                then(v.tensor_tensor(xo, xo, odiv[:, :, 0:DH], ALU.add))

            def gate(c, unit):
                norm(c, unit)
                dve.wait_ge(ev["sc"], unit - C + 1)
                fw = first_w[:, :].unsqueeze(1).to_broadcast([P, CT, E0])
                src = sc
                for r in range(2):
                    then(v.tensor_reduce(gst[:, r, :], src[:, :, :], AX_X, ALU.max))
                    then(v.tensor_tensor(key[:, :, :], src[:, :, :], more(gst[:, r, :], E0), ALU.is_equal))
                    then(v.tensor_tensor(key[:, :, :], key[:, :, :], fw, ALU.mult))
                    then(v.tensor_reduce(gst[:, 4, :], key[:, :, :], AX_X, ALU.max))
                    then(v.tensor_tensor(oh[:, r, :, :], key[:, :, :], more(gst[:, 4, :], E0), ALU.is_equal))
                    if r == 0:
                        then(v.scalar_tensor_tensor(sc2[:, :, :], oh[:, 0, :, :], NEG, sc[:, :, :], ALU.mult,
                                                    ALU.add))
                        src = sc2
                v.tensor_tensor(gst[:, 2, :], gst[:, 1, :], gst[:, 0, :], ALU.subtract).then_inc(s_gap, 1)
                dve.wait_ge(s_gex, unit - C + 1)
                then(v.tensor_scalar(gst[:, 5, :], gst[:, 3, :], 1.0, None, ALU.add))
                then(v.reciprocal(gst[:, 6, :], gst[:, 5, :]))
                then(v.tensor_tensor(gst[:, 7, :], gst[:, 3, :], gst[:, 6, :], ALU.mult))
                v.tensor_tensor(key[:, :, :], oh[:, 1, :, :], more(gst[:, 7, :], E0), ALU.mult)
                then(v.tensor_tensor(sc2[:, :, :], oh[:, 0, :, :], more(gst[:, 6, :], E0), ALU.mult))
                v.tensor_tensor(comb[:, :, :], key[:, :, :], sc2[:, :, :], ALU.add).then_inc(s_comb, 1)

            dve.wait_ge(ev["mask"], 2 * CT)
            dve.wait_ge(ev["rows"], H)
            dve.wait_ge(s_u, 1)
            for h in range(H):
                indicate(0, h)
                if h:
                    merge(0, h - 1)
            dve.wait_ge(ev["mask"], 2 * T)
            per = {"dve": 4 * 6 + 5 + 11 + 3 + 1}
            with dve.Fori(1, C) as c:
                k.enter(c, 1, per)
                dve.wait_ge(ev["rows"], c * H + H)
                indicate(c, 0)
                merge(c - 1, H - 1)
                gate(c - 1, c - 1 + C)
                for h in range(1, H):
                    indicate(c, h)
                    merge(c, h - 1)
                k.leave(C - 1, per)
            merge(C - 1, H - 1)
            gate(C - 1, 2 * C - 1)

            dve.wait_ge(s_acc, FFN_Y)
            replicate(1)
            norms(2 * C)
            dve.wait_ge(ev["proj"], 4 * C)
            S1, D1 = whx1[:, :, P:P + H], whx1[:, :, P + H:P + 2 * H]
            v.reduce_sum(dsum[:, :], D1, AX_X)
            then(v.scalar_tensor_tensor(zt[:, :, :], D1, -1.0, S1, ALU.mult, ALU.max))
            v.tensor_reduce(pmax[:, H:H + 1], dsum[:, :], AX_X, ALU.max)
            v.tensor_reduce(pmax[:, 0:H], zt[:, :, :].rearrange("p t h -> p h t"), AX_X,
                            ALU.max).then_inc(s_pm, 1)
            dve.wait_ge(s_gm, 2)
            v.tensor_scalar(nmx[:, 0:H], gmax[:, 1, 0:H], -SLOPE, None, ALU.mult)
            v.tensor_scalar(nmx[:, H:H + 1], gmax[:, 1, H:H + 1], -1.0 / H, None, ALU.mult).then_inc(s_arg, 1)
            dve.wait_ge(s_exp, 3)
            v.tensor_tensor(v1[:, :, 0:P], whx1[:, :, 0:P], v1[:, :, P:P + 1].to_broadcast([P, T, P]),
                            ALU.mult).then_inc(s_u, 1)

            def probabilities(c, first, quads):
                cs = bass.ts(c, CW)
                for q in quads:
                    if q >= 2:
                        dve.wait_ge(s_probf, c * (Q - 1) + (q - 1))
                    elif not first:
                        if q == 0:
                            dve.wait_ge(s_probf, c * (Q - 1))
                        else:
                            dve.wait_ge(full[1], c + C * H)
                    for h in range(H):
                        for j in range(QT):
                            t = q * QT + j
                            if h:
                                dve.wait_ge(s_step, c * (T * (H - 1)) + (q * QT * (H - 1) + (h - 1) * QT + j + 1))
                            last = v.scalar_tensor_tensor(
                                prob[:, t % 8, :], rows1[:, bass.ds((c % 2 * H + h) * CW, CW)], nd[:, t, h:h + 1],
                                maskT[:, t, cs] if h == 0 else prob[:, t % 8, :], ALU.max, ALU.mult)
                            last.then_inc(s_step if h < H - 1 else s_prob, 1)

            def merge1(c):
                dve.wait_ge(ev["att"], c * 2 + (2 * C * H + 2))
                a3 = att[:, 0:CT * (P + 1)].rearrange("p (t v) -> p t v", v=P + 1)
                then(v.reciprocal(rden[:, :], a3[:, :, P]))
                v.tensor_tensor(odiv[:, :, :], a3[:, :, 0:P], more(rden[:, :], P), ALU.mult).then_inc(s_attf, 1)
                dve.wait_ge(s_attf, c + (C * H + 1))
                xo = x[:, bass.ts(c, CT), :]
                then(v.tensor_tensor(xo, xo, odiv[:, :, :], ALU.add))

            dve.wait_ge(ev["rows"], H * (C + 2))
            probabilities(0, True, range(Q))
            per = {"dve": 7}
            with dve.Fori(1, C) as c:
                k.enter(c, 1, per)
                dve.wait_ge(ev["rows"], c * H + H * (C + 2))
                probabilities(c, False, range(1))
                merge1(c - 1)
                norm(c - 1, c - 1 + 3 * C)
                probabilities(c, False, range(1, Q))
                k.leave(C - 1, per)
            merge1(C - 1)
            norm(C - 1, 4 * C - 1)


def kernel(**inputs):
    import concourse.bacc as bacc
    from concourse.bass_utils import run_bass_kernel_spmd

    w = {n: np.asarray(v) for n, v in inputs.items()}
    lay = {
        "x": w["x"], "adj": w["adj"],
        "gW0": w["L0_gnn_W"], "gWT0": w["L0_gnn_W"].T, "gb0": w["L0_gnn_b"].reshape(1, P), "ga0": w["L0_gnn_a"],
        "gW1": w["L1_gnn_W"], "gWT1": w["L1_gnn_W"].T, "ga1": w["L1_gnn_a"].reshape(1, 2 * DH),
        "wgT": w["L0_ffn_Wg"].T, "bg": w["L0_ffn_bg"].reshape(1, E0),
        "w1T": w["L0_ffn_W1"].transpose(2, 0, 1),
        "b1": w["L0_ffn_b1"].reshape(E0, HC, P).transpose(2, 0, 1),
        "w2T": w["L0_ffn_W2"].reshape(E0, P, HC, P).transpose(3, 0, 2, 1), "b2": w["L0_ffn_b2"],
        "route": w["L1_ffn_route_id"].reshape(1, N // GRP),
        "wiT": w["L1_ffn_Wi"].T, "bi": w["L1_ffn_bi"].reshape(KC, P).T,
        "wrT": w["L1_ffn_Wr"].reshape(L, E1, HID, KC, P).transpose(4, 0, 1, 3, 2).reshape(P, L, E1, KC * HID),
        "br": w["L1_ffn_br"].transpose(1, 0, 2),
        "wsT": w["L1_ffn_Ws"].reshape(L, HID, KC, P).transpose(3, 0, 2, 1).reshape(P, L, KC * HID),
        "bs": w["L1_ffn_bs"].reshape(1, L, HID),
        "woT": w["L1_ffn_Wo"].reshape(P, KC, P).transpose(2, 1, 0), "bo": w["L1_ffn_bo"].reshape(1, P),
    }
    nc = bacc.Bacc("TRN2", target_bir_lowering=False, num_devices=1)
    arrays, args = {}, {}
    for name, v in lay.items():
        v = np.ascontiguousarray(v)
        arrays[f"in_{name}"] = v
        args[name] = nc.dram_tensor(f"in_{name}", v.shape, mybir.dt.from_np(v.dtype), kind="ExternalInput").ap()
    out = nc.dram_tensor("out_x", (N, P), F32, kind="ExternalOutput").ap()
    gnn_moe_stack(nc, args, out)
    r = run_bass_kernel_spmd(nc, [arrays], core_ids=[0])
    return r.results[0]["out_x"]
```

```python
from contextlib import ExitStack

import numpy as np

import concourse.bass as bass
from concourse import mybir

ALU = mybir.AluOpType
ACT = mybir.ActivationFunctionType
F32 = mybir.dt.float32
BF16 = mybir.dt.bfloat16
I32 = mybir.dt.int32
AX_X = mybir.AxisListType.X
RMAX = bass.bass_isa.ReduceOp.max

P = 128
N = 2048
T = N // P
CT = 4
C = T // CT
CW = CT * P
H = 4
DH = P // H
V1 = DH + 1
PARTS = 3
VW = PARTS * V1
QT = 4
Q = T // QT
E0 = 8
HC = 4
E1 = 16
HID = 256
KC = HID // P
L = 2
GRP = 32
GT = P // GRP
EPS = 1e-5
SLOPE = 0.2
BIG = 2.0 ** 40
SHIFT = 60.0
LIFT = 15.0
NEG = -3.0e38
XC = P + 2 * H
XM = XC + 1


class Count:

    def __init__(self):
        self.n, self.off, self.bank = {}, {}, {}

    def event(self, name, by=1):
        self.n[name] = self.n.get(name, 0) + by
        return self.at(name)

    def at(self, name):
        return self.off.get(name, 0) + self.n.get(name, 0)

    def fill(self, b, name):
        self.event(name)
        self.bank[b] = (name, self.n[name])

    def freed(self, b):
        name, n = self.bank[b]
        return name, self.off.get(name, 0) + n

    def enter(self, i, first, per):
        self.at_entry = dict(self.n), dict(self.off), dict(self.bank)
        for name, by in per.items():
            self.off[name] = (i - first) * by + self.off.get(name, 0)

    def leave(self, turns, per):
        n0, off0, bank0 = self.at_entry
        made = {name: n - n0.get(name, 0) for name, n in self.n.items() if n != n0.get(name, 0)}
        assert made == per, (made, per)
        for b, (name, n) in self.bank.items():
            assert bank0.get(b) in ((name, n), (name, n - per.get(name, 0))), (b, name)
        for name, by in per.items():
            self.off[name] = (turns - 1) * by + off0.get(name, 0)


def gnn_moe_stack(nc, a, out):
    with ExitStack() as ctx:
        def sb(name, shape, dt=F32):
            return ctx.enter_context(nc.sbuf_tensor(name, shape, dt))

        def sem(name):
            return ctx.enter_context(nc.semaphore(name))

        maskT = sb("maskT", [P, T, N], BF16)
        x = sb("x", [P, T, P])
        hT = sb("hT", [P, N])
        hTc = sb("hTc", [P, CW])
        xn = sb("xn", [P, CT, P])
        odiv = sb("odiv", [P, CT, P])
        sbc = sb("sbc", [P, H, CW])
        att = sb("att", [P, CT * 2 * VW])
        ysb = sb("ysb", [P, 3, CW])
        arena = sb("arena", [P, 12288])
        wnat = [arena[:, s * P:(s + 1) * P] for s in range(2)]
        brep = arena[:, 2 * P:3 * P]
        brow = att[:, 0:P]
        ind = arena[:, 0:8192].bitcast(BF16).rearrange("p (q b j i) -> p q b j i", q=Q, b=2, j=QT)
        uf = maskT[:, :, N - 4 * H * V1:N].bitcast(F32).rearrange("p t (h b v) -> p t h b v", h=H, b=2)
        whx0 = arena[:, 8192:8192 + T * XC].rearrange("p (t k) -> p t k", t=T)
        w1 = arena[:, 8192:10240].rearrange("p (s e f) -> p s e f", s=2, e=2)
        w2 = arena[:, 10240:12288].rearrange("p (s e c d) -> p s e c d", s=2, e=2, c=HC)
        whx1 = arena[:, 0:T * XM].rearrange("p (t k) -> p t k", t=T)
        prob0 = arena[:, 4096:8192].rearrange("p (s i) -> p s i", s=8)
        wsel = arena[:, 0:8192].rearrange("p (s k n) -> p s k n", s=2 * L * GT, k=KC)
        at = [8192]

        def in_arena(parts, *dims):
            n = int(np.prod(dims))
            at[0] += n
            return arena[0:parts, at[0] - n:at[0]]

        wiT = in_arena(P, HID)
        bi = in_arena(P, KC)
        ws = in_arena(P, L, KC * HID).rearrange("p (l n) -> p l n", l=L)
        brs = in_arena(E1, L, HID).rearrange("p (l n) -> p l n", l=L)
        bsr = in_arena(E1, L, HID).rearrange("p (l n) -> p l n", l=L)
        woT = in_arena(P, KC, P).rearrange("p (k n) -> p k n", k=KC)
        bo = in_arena(1, P)
        tiles1 = sbc[:, :, :].rearrange("p h i -> p (h i)")
        htt = tiles1[:, 0:6 * HID].rearrange("p (r l n) -> p r l n", r=2, l=L + 1)
        hn = tiles1[:, 6 * HID:8 * HID].rearrange("p (r n) -> p r n", r=2)
        reg_b = sb("reg_b", [P, T * H * 2 * VW // 2])
        u = reg_b[:, :].bitcast(BF16).rearrange("p (g s v) -> p g s v", s=PARTS, v=V1)
        u6 = u.rearrange("p (t h b) s v -> p t h b s v", t=T, h=H)
        v1 = reg_b[:, 0:T * (P + 1)].rearrange("p (t v) -> p t v", t=T)
        rows1 = reg_b[:, T * (P + 1):T * (P + 1) + 2 * H * CW]
        reg_c = sb("reg_c", [P, 4096])
        adj = reg_c[:, :].bitcast(BF16).rearrange("p (s j) -> p s j", s=4)
        hid = reg_c[:, :].rearrange("p (e c i) -> p e c i", e=2, c=HC)
        prob = reg_c[:, :].rearrange("p (s i) -> p s i", s=8)
        wxs = [sb(f"wx{s}", [P, XM]) for s in range(2)]
        wsq = sb("wsq", [P, 2 * H + 1])
        wnorm = sb("wnorm", [P, 2 * H + 1])
        asel = [sb(f"asel{s}", [P, 2 * H]) for s in range(2)]
        wrep = sb("wrep", [P, H, P])
        ident = sb("ident", [P, P])
        identb = sb("identb", [P, P], BF16)
        ones = sb("ones", [P, P])
        consts = sb("consts", [P, 4])
        bcol = sb("bcol", [P, 1])
        bac = sb("bac", [P, 2 * H])
        bsum = sb("bsum", [P, H])
        gb = sb("gb", [P, H])
        halves = sb("halves", [P, T, 6])
        means = sb("means", [P, T])
        waited = sb("waited", [P, 1])
        var = sb("var", [P, T])
        nhalf = sb("nhalf", [P, T])
        step = sb("step", [P, T])
        rstd = sb("rstd", [P, T])
        nd = sb("nd", [P, T, H])
        thr = sb("thr", [P, QT, H])
        dsh = sb("dsh", [P, T, H])
        bd = sb("bd", [P, T, H, 2])
        ab = sb("ab", [P, T, H, 2])
        arg = sb("arg", [P, T, H, 2])
        zt = sb("zt", [P, T, H])
        zm = sb("zm", [P, T, H])
        pmax = sb("pmax", [P, H])
        gmax = sb("gmax", [P, H])
        nmx = sb("nmx", [P, H + 1])
        red = sb("red", [P, 2 * CT, V1])
        wred = sb("wred", [P, 2 * CT, V1])
        num = sb("num", [P, CT, V1])
        rden = sb("rden", [P, CT])
        wgT = sb("wgT", [P, E0])
        bg = sb("bg", [1, E0])
        b1 = sb("b1", [P, E0, HC])
        b2 = sb("b2", [E0, P])
        sc = sb("sc", [P, CT, E0])
        sc2 = sb("sc2", [P, CT, E0])
        first_i = sb("first_i", [P, E0], I32)
        first_w = sb("first_w", [P, E0])
        oh = sb("oh", [P, 2, CT, E0])
        key = sb("key", [P, CT, E0])
        gst = sb("gst", [P, 8, CT])
        comb = sb("comb", [P, CT, E0])
        ohx = sb("ohx", [E1, CW])
        combT = ohx[0:E0, :].rearrange("e (t i) -> e t i", t=CT)
        route = sb("route", [1, N // GRP], I32)
        route16 = sb("route16", [E1, N // GRP], I32)
        routef = sb("routef", [E1, N // GRP])
        chan_i = sb("chan_i", [E1, 1], I32)
        chan = sb("chan", [E1, 1])
        onehot = sb("onehot", [E1, N // GRP])

        bank = [ctx.enter_context(nc.psum_tensor(f"bank{b}", [P, 512], F32)) for b in range(8)]
        bankb = [t[:, :].bitcast(BF16) for t in bank]

        full = [sem(f"bank{b}_full") for b in range(8)]
        s_x = [sem(f"x_chunk{c}_loaded") for c in range(C)]
        s_w = sem("first_projection_loaded")
        s_w2 = sem("small_weights_loaded")
        s_wp = [sem(f"expert_pair_slot{r}_loaded") for r in range(2)]
        s_w1 = sem("second_mixture_loaded")
        s_adj = [sem(f"adj_slot{r}_loaded") for r in range(4)]
        s_sel = [sem(f"selected_weights_slot{r}_loaded") for r in range(2 * L * GT)]
        s_const = sem("constants_ready")
        s_pool = sem("gpsimd_step_done")
        s_dve = sem("vector_step_done")
        s_brep = sem("bias_replicated")
        s_rep = sem("replicated_score_weights_ready")
        s_wsq = sem("score_weights_squared")
        s_nmx = sem("score_bounds_ready")
        s_xn = sem("chunk_normalised")
        s_pm = sem("partition_maxima_ready")
        s_gm = sem("global_maxima_ready")
        s_arg = sem("exponents_ready")
        s_exp = sem("exponentials_ready")
        s_xb = sem("bias_added_to_chunk")
        s_split = sem("gpsimd_split_step_done")
        s_u = sem("values_ready")
        s_above = sem("scaled_logits_ready")
        s_g = sem("indicator_above_ready")
        s_ind = sem("indicator_quad_ready")
        s_indf = sem("indicator_quad_used")
        s_attf = sem("attention_sums_used")
        s_gap = sem("gate_gap_ready")
        s_gex = sem("gate_exp_ready")
        s_comb = sem("combine_weights_ready")
        s_acc = sem("weighted_output_added")
        s_step = sem("product_step_done")
        s_prob = sem("probability_tile_ready")
        s_prob0 = sem("chunk0_probability_tile_ready")
        s_probf = sem("probability_quad_used")
        s_wc = sem("shared_weights_summed")
        s_ohx = sem("onehot_chunk_ready")
        s_out = sem("output_stored")
        ev = {name: sem(what) for name, what in (
            ("ext", "score_weights_ready"), ("mask", "mask_half_row_ready"), ("hTc", "chunk_transposed"),
            ("proj", "projected_half_chunk_ready"), ("rows", "source_row_ready"), ("att", "attention_sums_ready"),
            ("sc", "gate_scores_ready"), ("combT", "combine_weights_transposed"), ("hid", "hidden_block_ready"),
            ("y", "weighted_output_ready"), ("htt", "hidden_tile_ready"),
            ("bound", "weight_norms_ready"))}
        NW = 4 + 2 * H + 2
        NW2 = 6
        NW1 = 7
        NC = 8
        ROWS = (range(6, 8), range(8, 10), range(10, 13), range(13, T))
        HB = (2, 3, 6, 7)
        BANK3 = 2 * C + C * E0
        BANK5 = C * (E0 // 2 + 1)
        FFN_Y = C * (E0 + 1)
        block = ctx.enter_context(nc.Block())

        def more(ap, n):
            return ap.unsqueeze(len(ap.shape)).to_broadcast([*ap.shape, n])

        def split(engine, h, then):
            f = uf[:, :, h, :, :]
            for b in range(2):
                engine.tensor_tensor(uf[:, :, h, b, 0:DH], whx0[:, :, h * DH:(h + 1) * DH],
                                     more(bd[:, :, h, b], DH), ALU.mult)
            then(engine.tensor_copy(uf[:, :, h, :, DH], bd[:, :, h, :]))
            then(engine.tensor_copy(u6[:, :, h, :, 0, :], f))
            then(engine.tensor_tensor(f, f, u6[:, :, h, :, 0, :], ALU.subtract))
            then(engine.tensor_copy(u6[:, :, h, :, 1, :], f))
            if h:
                engine.wait_ge(s_u, h)
            engine.tensor_tensor(u6[:, :, h, :, 2, :], f, u6[:, :, h, :, 1, :], ALU.subtract).then_inc(s_u, 1)

        @block.sync
        def _(sp):
            xin = a["x"].rearrange("(t p) d -> p t d", p=P)
            for c in range(C):
                sp.dma_start(x[:, c * CT:(c + 1) * CT, :], xin[:, c * CT:(c + 1) * CT, :]).then_inc(s_x[c], 16)
            sp.wait_ge(s_const, NC)
            with nc.allow_non_contiguous_dma(reason="small vectors"):
                for s in range(2):
                    sp.dma_start(wnat[s], a[f"gW{s}"]).then_inc(s_w, 16)
                    sp.dma_start(wxs[s][:, 0:P], a[f"gWT{s}"]).then_inc(s_w, 16)
                for h in range(H):
                    for s in range(2):
                        src = a["ga0"][h:h + 1, :] if s == 0 else a["ga1"]
                        sp.dma_start(asel[s][h * DH:(h + 1) * DH, h:2 * H:H],
                                     src.rearrange("o (k d) -> (o d) k", k=2)).then_inc(s_w, 16)
                sp.dma_start(bcol[:, :], a["gb0"].rearrange("o k -> k o")).then_inc(s_w, 16)
            sp.dma_start(brow, a["gb0"].to_broadcast([P, P])).then_inc(s_w, 16)
            sp.dma_start(wgT[:, :], a["wgT"]).then_inc(s_w2, 16)
            sp.dma_start(bg[:, :], a["bg"]).then_inc(s_w2, 16)
            sp.dma_start(b1[:, :, :], a["b1"]).then_inc(s_w2, 16)
            sp.dma_start(b2[:, :], a["b2"]).then_inc(s_w2, 16)
            sp.dma_start(route[:, :], a["route"]).then_inc(s_w2, 16)
            sp.dma_start(route16[:, :], a["route"].to_broadcast([E1, N // GRP])).then_inc(s_w2, 16)
            sp.wait_ge(s_u, H)
            sp.wait_ge(s_arg, 2)

            def load_pair(c, h, wait):
                if wait:
                    sp.wait_ge(full[5], c * (H + 1) + (h if h >= 2 else h - 1))
                e = slice(2 * h, 2 * h + 2)
                sp.dma_start(w1[:, h % 2, :, :], a["w1T"][:, e, :]).then_inc(s_wp[h % 2], 16)
                sp.dma_start(w2[:, h % 2, :, :, :], a["w2T"][:, e, :, :]).then_inc(s_wp[h % 2], 16)

            for h in range(H):
                load_pair(0, h, h >= 2)
            with sp.Fori(1, C) as c:
                for h in range(H):
                    load_pair(c, h, True)
            sp.wait_ge(s_acc, FFN_Y)
            sp.dma_start(wiT, a["wiT"]).then_inc(s_w1, 16)
            sp.dma_start(bi, a["bi"]).then_inc(s_w1, 16)
            sp.dma_start(ws, a["wsT"]).then_inc(s_w1, 16)
            sp.dma_start(brs, a["br"]).then_inc(s_w1, 16)
            sp.dma_start(bsr, a["bs"].to_broadcast([E1, L, HID])).then_inc(s_w1, 16)
            sp.dma_start(woT, a["woT"]).then_inc(s_w1, 16)
            sp.dma_start(bo, a["bo"]).then_inc(s_w1, 16)

            def select(pair, wait):
                for r in range(2):
                    for l in range(L):
                        for g in range(GT):
                            s = (r * L + l) * GT + g
                            e = sp.value_load(route[0:1, bass.ds(pair * 2 * GT + r * GT + g, 1)], min_val=0,
                                              max_val=E1 - 1)
                            if wait:
                                sp.wait_ge(full[3 + 2 * r],
                                           (pair - 1) * (L + 1) + ((BANK5 if r else BANK3) + l + 1))
                            elif (r, l, g) == (1, 0, 0):
                                sp.wait_ge(full[1], C * H + 1)
                            sp.dma_start(wsel[:, s, :, :].rearrange("p k n -> p (k n)").unsqueeze(1),
                                         a["wrT"][:, l, bass.ds(e, 1), :]).then_inc(s_sel[s], 16)

            sp.wait_ge(s_u, H + C)
            sp.wait_ge(s_exp, 2 + C)
            select(0, False)
            with sp.Fori(1, T // 2) as pair:
                select(pair, True)

        @block.gpsimd
        def _(pool):
            nc.gpsimd.memset(ident[:, :], 0.0).then_inc(s_pool, 1)
            for m in (asel[0], asel[1]):
                nc.gpsimd.memset(m[:, :], 0.0).then_inc(s_const, 1)
            nc.gpsimd.memset(ones[:, :], 1.0).then_inc(s_const, 1)
            for i, v in enumerate((SHIFT, SLOPE * SHIFT, -SHIFT, -SLOPE * SHIFT)):
                last = nc.gpsimd.memset(consts[:, i:i + 1], v)
            last.then_inc(s_const, 1)
            nc.gpsimd.iota(first_i[:, :], pattern=[[-1, E0]], base=E0, channel_multiplier=0).then_inc(s_pool, 1)
            nc.gpsimd.iota(chan_i[:, :], pattern=[[0, 1]], base=0, channel_multiplier=1).then_inc(s_pool, 1)
            pool.wait_ge(s_pool, 3)
            nc.gpsimd.affine_select(out=ident[:, :], in_=ident[:, :], compare_op=ALU.not_equal, fill=1.0,
                                    base=0, pattern=[[-1, P]], channel_multiplier=1).then_inc(s_pool, 1)
            nc.gpsimd.tensor_copy(first_w[:, :], first_i[:, :]).then_inc(s_const, 1)
            nc.gpsimd.tensor_copy(chan[:, :], chan_i[:, :]).then_inc(s_const, 1)
            pool.wait_ge(s_pool, 4)
            nc.gpsimd.tensor_copy(identb[:, :], ident[:, :]).then_inc(s_const, 1)
            nc.gpsimd.memset(pmax[:, :], 0.0).then_inc(s_const, 1)

            def load_rows(r):
                if r >= 4:
                    pool.wait_ge(full[7], r - 3 + (0 if r < 8 else 2 if r < 12 else 3))
                pool.dma_start(adj[:, r % 4, :], a["adj"][r * P:(r + 1) * P, :]).then_inc(s_adj[r % 4], 16)

            for r in range(8):
                load_rows(r)
            pool.wait_ge(s_w, 16 * NW)
            for c in range(C):
                pool.wait_ge(s_xn, c + 1)
                xi = x[:, c * CT:(c + 1) * CT, :]
                nc.gpsimd.tensor_tensor(xi, xi, brow.unsqueeze(1).to_broadcast([P, CT, P]),
                                        ALU.add).then_inc(s_xb, 1)
            pool.wait_ge(s_pm, 1)
            nc.gpsimd.partition_all_reduce(gmax[:, :], pmax[:, :], P, RMAX).then_inc(s_gm, 1)
            pool.wait_ge(s_exp, 1)
            k = Count()

            def then(ins):
                ins.then_inc(s_split, 1)
                pool.wait_ge(s_split, k.event("split"))

            for h in range(1, H):
                split(nc.gpsimd, h, then)
                for r in {1: range(8, 10), 2: range(10, 12), 3: range(12, T)}[h]:
                    load_rows(r)

            for n in range(FFN_Y):
                c, e = divmod(n, E0 + 1)
                pool.wait_ge(ev["y"], n + 1)
                if e:
                    pool.wait_ge(s_acc, n)
                xi = x[:, c * CT:(c + 1) * CT, :]
                nc.gpsimd.tensor_tensor(xi, xi, ysb[:, e % 3, :].rearrange("p (t d) -> p t d", d=P),
                                        ALU.add).then_inc(s_acc, 1)
                if c == C - 1 and e in (2, 3, 5, E0):
                    g = (2, 3, 5, E0).index(e)
                    tiles = slice(g * CT, (g + 1) * CT)
                    pool.wait_ge(s_exp, 3 + g)
                    nc.gpsimd.tensor_tensor(v1[:, tiles, 0:P], whx1[:, tiles, 0:P],
                                            v1[:, tiles, P:P + 1].to_broadcast([P, CT, P]),
                                            ALU.mult).then_inc(s_u, 1)
            pool.wait_ge(s_w2, 16 * NW2)
            nc.gpsimd.tensor_copy(routef[:, :], route16[:, :]).then_inc(s_pool, 1)
            pool.wait_ge(s_pool, 5)
            nc.gpsimd.tensor_scalar(onehot[:, :], routef[:, :], chan[:, 0:1], None,
                                    ALU.is_equal).then_inc(s_pool, 1)
            pool.wait_ge(s_w1, 16 * NW1)
            nc.gpsimd.tensor_tensor(brs, brs, bsr, ALU.add).then_inc(s_wc, 1)
            for l in range(L):
                for kc in range(KC):
                    d = ws[:, l, kc * HID + kc * P:kc * HID + (kc + 1) * P]
                    nc.gpsimd.tensor_tensor(d, d, ident[:, :], ALU.add).then_inc(s_wc, 1)
            pool.wait_ge(s_pool, 6)
            outv = out.rearrange("(t p) d -> p t d", p=P)
            for c in range(C):
                nc.gpsimd.tensor_copy(ohx[:, :].rearrange("e (g i) -> e g i", i=GRP),
                                      more(onehot[:, c * CT * GT:(c + 1) * CT * GT], GRP)).then_inc(s_ohx, 1)
                for i in range(CT):
                    pool.wait_ge(ev["y"], FFN_Y + c * CT + i + 1)
                    xi = x[:, c * CT + i, :]
                    nc.gpsimd.tensor_tensor(xi, xi, ysb[:, 0, i * P:(i + 1) * P], ALU.add).then_inc(s_acc, 1)
                pool.wait_ge(s_acc, FFN_Y + c * CT + CT)
                pool.dma_start(outv[:, c * CT:(c + 1) * CT, :],
                               x[:, c * CT:(c + 1) * CT, :]).then_inc(s_out, 16)
            pool.wait_ge(s_out, 16 * C)

        @block.tensor
        def _(pe):
            k = Count()
            mm = nc.tensor.matmul

            def use(b, event):
                if b in k.bank:
                    name, v = k.freed(b)
                    pe.wait_ge(ev[name], v)
                k.fill(b, event)

            def ln_transpose(b=6, src=xn):
                pe.wait_ge(s_xn, k.event("xn"))
                use(b, "hTc")
                for i in range(CT):
                    last = nc.tensor.transpose(bank[b][:, i * P:(i + 1) * P], src[:, i, :], ident[:, :])
                last.then_inc(full[b], 1)

            def normalised():
                pe.wait_ge(ev["hTc"], k.at("hTc"))

            def mask_rows(r):
                pe.wait_ge(s_adj[r % 4], 16 * (r // 4 + 1))
                for half in range(2):
                    b = 6 + half
                    use(b, "mask")
                    for j in range(T // 2):
                        jt = half * T // 2 + j
                        last = nc.tensor.transpose(bankb[b][:, j * P:(j + 1) * P],
                                                   adj[:, r % 4, jt * P:(jt + 1) * P], identb[:, :])
                    last.then_inc(full[b], 1)

            def project(s, c):
                normalised()
                for i in range(CT):
                    b = 2 + i // 2
                    if i % 2 == 0:
                        use(b, "proj")
                    t = c * CT + i
                    last = mm(bank[b][:, (i % 2) * XM:(i % 2) * XM + XC + s], hT[:, t * P:(t + 1) * P],
                              wxs[s][:, 0:XC + s], start=True, stop=True)
                    if i % 2:
                        last.then_inc(full[b], 1)

            def source_row(h, c):
                b = 6 + h % 2
                use(b, "rows")
                mm(bank[b][:, :], wrep[:, h, :], hT[:, bass.ts(c, CW)], start=True,
                   stop=True).then_inc(full[b], 1)

            def attend(h):
                use(0, "att")
                use(1, "att")
                for q in range(Q):
                    pe.wait_ge(s_ind, k.event("ind"))
                    for j in range(QT):
                        t = q * QT + j
                        for i in range(CT):
                            for b in range(2):
                                o = (i % 2) * 2 * VW + b * VW
                                last = mm(bank[i // 2][:, o:o + VW], ind[:, q, b, j, i * P:(i + 1) * P],
                                          u[:, (t * H + h) * 2 + b, :, :],
                                          start=(t == 0 and i % 2 == 0 and b == 0), stop=(t == T - 1),
                                          skip_group_check=True)
                            if t == T - 1 and i % 2:
                                last.then_inc(full[i // 2], 1)
                    if q < Q - 1:
                        last.then_inc(s_indf, 1)

            def scores():
                ln_transpose()
                normalised()
                use(4, "sc")
                for i in range(CT):
                    o = bank[4][:, i * E0:(i + 1) * E0]
                    mm(o, hTc[:, i * P:(i + 1) * P], wgT[:, :], start=True, stop=False)
                    last = mm(o, ones[0:1, :], bg[:, :], start=False, stop=True)
                last.then_inc(full[4], 1)

            def combine():
                pe.wait_ge(s_comb, k.event("comb"))
                use(6, "combT")
                for i in range(CT):
                    last = nc.tensor.transpose(bank[6][0:E0, i * P:(i + 1) * P], comb[:, i, :], ident[:, :])
                last.then_inc(full[6], 1)
                pe.wait_ge(ev["combT"], k.at("combT"))
                use(5, "y")
                for i in range(CT):
                    last = mm(bank[5][:, i * P:(i + 1) * P], combT[:, i, :], b2[:, :], start=True, stop=True)
                last.then_inc(full[5], 1)

            def first_layer(pair):
                s = pair % 2
                pe.wait_ge(s_wp[s], k.event(f"pair{s}", 32))
                for e in (2 * pair, 2 * pair + 1):
                    for c in range(HC):
                        b = HB[c]
                        use(b, "hid")
                        mm(bank[b][:, :], w1[:, s, e % 2, c * P:(c + 1) * P], hTc[:, :], start=True,
                           stop=True).then_inc(full[b], 1)

            def second_layer(pair):
                s = pair % 2
                for e in (2 * pair, 2 * pair + 1):
                    b = 4 + e % 2
                    use(b, "y")
                    pe.wait_ge(ev["hid"], k.at("hid") - (HC if e % 2 == 0 else 0))
                    for i in range(CT):
                        for c in range(HC):
                            last = mm(bank[b][:, i * P:(i + 1) * P], hid[:, e % 2, c, i * P:(i + 1) * P],
                                      w2[:, s, e % 2, c, :], start=(c == 0), stop=(c == HC - 1))
                    last.then_inc(full[b], 1)

            pe.wait_ge(s_const, NC)
            for r in range(CT):
                mask_rows(r)
            pe.wait_ge(s_w, 16 * NW)
            pe.wait_ge(s_brep, 1)
            use(6, "ext")
            mm(bank[6][:, 0:8], wnat[0], asel[0][:, :], start=True, stop=True)
            mm(bank[6][:, 8:16], wnat[1], asel[1][:, :], start=True, stop=True)
            mm(bank[6][:, 16:24], brep, asel[0][:, :], start=True, stop=True).then_inc(full[6], 1)
            for c in range(C):
                ln_transpose((6, 4)[c % 2], (xn, odiv)[c % 2])
                project(0, c)
            pe.wait_ge(s_rep, H)
            for h in range(H):
                source_row(h, 0)
            pe.wait_ge(s_wsq, 1)
            use(6, "bound")
            mm(bank[6][:, 0:2 * H + 1], ones[:, :], wsq[:, :], start=True, stop=True).then_inc(full[6], 1)
            for r in range(CT, CT + 2):
                mask_rows(r)
            for h in range(H):
                pe.wait_ge(s_u, h + 1)
                attend(h)
                source_row(h, 1)
                for r in ROWS[h]:
                    mask_rows(r)

            def chunk0(next_rows):
                scores()
                first_layer(0)
                for h in range(H):
                    attend(h)
                    source_row(h, next_rows)
                    if h:
                        first_layer(h)
                    second_layer(h)
                    if h == 0:
                        combine()

            pe.wait_ge(s_w2, 16 * NW2)
            chunk0(2)
            per = {"att": 8, "ind": 16, "rows": 4, "xn": 1, "hTc": 1, "sc": 1, "comb": 1, "combT": 1,
                   "hid": 32, "y": 9, "pair0": 64, "pair1": 64}
            with pe.Fori(2, C) as c:
                k.enter(c, 2, per)
                chunk0((c + 1) % C)
                k.leave(C - 2, per)
            def attend1(t, prob=prob, ready=s_prob):
                if t == 0:
                    use(0, "att")
                    use(1, "att")
                pe.wait_ge(ready, k.event("prob0" if ready is s_prob0 else "prob"))
                for i in range(CT):
                    b, o = (0, i * (P + 1)) if i < 3 else (1, 0)
                    last = mm(bank[b][:, o:o + P + 1], prob[:, t % 8, i * P:(i + 1) * P], v1[:, t, :],
                              start=(t == 0 and i in (0, 3)), stop=(t == T - 1), skip_group_check=True)
                    if t == T - 1 and i >= 2:
                        last.then_inc(full[b], 1)
                if t % QT == QT - 1 and t < T - 1:
                    last.then_inc(s_probf, 1)

            def ready(b):
                name, v = k.freed(b)
                pe.wait_ge(ev[name], v)

            def hidden(i):
                b = 2 + i % 2 * 2
                use(b, "htt")
                for m in range(KC):
                    last = mm(bank[b][:, m * P:(m + 1) * P], wiT[:, m * P:(m + 1) * P],
                              hTc[:, i * P:(i + 1) * P], start=True, stop=True)
                last.then_inc(full[b], 1)

            def layer(i, l):
                r, b = i % 2, 3 + i % 2 * 2
                o = bank[b][:, 0:HID]
                use(b, "htt")
                mm(o, ohx[:, i * P:(i + 1) * P], brs[:, l, :], start=True, stop=False, skip_group_check=True)
                ready(b - 1)
                for kc in range(KC):
                    mm(o, htt[:, r, l, kc * P:(kc + 1) * P], ws[:, l, kc * HID:(kc + 1) * HID],
                       start=False, stop=False, skip_group_check=True)
                for g in range(GT):
                    s = (r * L + l) * GT + g
                    pe.wait_ge(s_sel[s], k.event(f"sel{r}{l}{g}", 16))
                    for kc in range(KC):
                        c = kc * P + g * GRP
                        last = mm(bank[b][g * GRP:(g + 1) * GRP, 0:HID], htt[:, r, l, c:c + GRP],
                                  wsel[:, s, kc, :], start=False, stop=(kc == KC - 1),
                                  skip_group_check=True, tile_position=(0, g * GRP))
                last.then_inc(full[b], 1)

            def turn(i):
                b = 2 + i % 2 * 2
                ready(b + 1)
                use(b, "htt")
                for kc in range(KC):
                    last = nc.tensor.transpose(bank[b][:, kc * P:(kc + 1) * P],
                                               hn[:, i % 2, kc * P:(kc + 1) * P], ident[:, :])
                last.then_inc(full[b], 1)

            def output(i):
                r, b = i % 2, 3 + i % 2 * 2
                ready(b - 1)
                use(b, "y")
                for kc in range(KC):
                    mm(bank[b][:, 0:P], htt[:, r, L, kc * P:(kc + 1) * P], woT[:, kc, :], start=(kc == 0),
                       stop=False)
                mm(bank[b][:, 0:P], ones[0:1, :], bo[:, :], start=False, stop=True).then_inc(full[b], 1)

            def prepare1(c):
                ln_transpose()
                project(1, c)
                if c == 0:
                    pe.wait_ge(s_rep, 2 * H)
                if c < 2:
                    for h in range(H):
                        source_row(h, c)

            def quad(q):
                pe.wait_ge(s_u, H + 1 + q)
                for t in range(q * QT, (q + 1) * QT):
                    attend1(t, prob0, s_prob0)

            scores()
            for h in range(H):
                if h == 3:
                    quad(0)
                first_layer(h)
                if h in (1, 2):
                    prepare1(h)
                second_layer(h)
                if h == 0:
                    combine()
                    prepare1(0)
            prepare1(3)
            for q in range(1, Q):
                quad(q)
            pe.wait_ge(s_wc, 1 + L * KC)

            def chunk1(next_rows):
                for t in range(QT):
                    attend1(t)
                ln_transpose()
                normalised()
                pe.wait_ge(s_ohx, k.event("ohx"))
                hidden(0)
                for i in range(CT):
                    for l in range(L):
                        layer(i, l)
                        attend1(QT + 3 * i + 2 * l)
                        if i == 0 and l == 0:
                            for h in range(H):
                                source_row(h, next_rows)
                        turn(i)
                        if l == 0:
                            attend1(QT + 3 * i + 1)
                    if i < CT - 1:
                        hidden(i + 1)
                    output(i)

            chunk1(2)
            per = {"att": 2, "prob": 16, "rows": 4, "xn": 1, "hTc": 1, "ohx": 1, "htt": 20, "y": 4}
            per.update({f"sel{r}{l}{g}": 32 for r in range(2) for l in range(L) for g in range(GT)})
            with pe.Fori(2, C) as c:
                k.enter(c, 2, per)
                chunk1((c + 1) % C)
                k.leave(C - 2, per)
            ln_transpose()
            normalised()
            pe.wait_ge(s_ohx, k.event("ohx"))
            for i in range(0, CT, 2):
                pair = (i, i + 1)
                for j in pair:
                    hidden(j)
                for l in range(L):
                    for j in pair:
                        layer(j, l)
                    for j in pair:
                        turn(j)
                for j in pair:
                    output(j)

        @block.scalar
        def _(act):
            k = Count()
            af = nc.scalar.activation

            def got(b):
                act.wait_ge(full[b], k.event(f"full{b}"))

            def ln_out(c=None, b=6):
                got(b)
                af(hTc[:, :] if c is None else hT[:, c * CW:(c + 1) * CW], bank[b][:, :],
                   ACT.Copy).then_inc(ev["hTc"], 1)

            def mask_rows(r):
                for half in range(2):
                    b = 6 + half
                    got(b)
                    af(maskT[:, half * 8:(half + 1) * 8, r * P:(r + 1) * P],
                       bankb[b].rearrange("p (j i) -> p j i", i=P), ACT.Copy).then_inc(ev["mask"], 1)

            def project(whx, c):
                for half in range(2):
                    b = 2 + half
                    got(b)
                    n = whx.shape[2]
                    af(whx[:, c * CT + 2 * half:c * CT + 2 * half + 2, :],
                       bank[b][:, 0:2 * XM].rearrange("p (t k) -> p t k", t=2)[:, :, 0:n],
                       ACT.Copy).then_inc(ev["proj"], 1)

            def source_row(h):
                got(6 + h % 2)
                af(sbc[:, h, :], bank[6 + h % 2][:, :], ACT.Copy).then_inc(ev["rows"], 1)

            def source_rows1(parity):
                for h in range(H):
                    got(6 + h % 2)
                    af(rows1[:, bass.ds((parity * H + h) * CW, CW)], bank[6 + h % 2][:, :], ACT.Exp,
                       bias=nmx[:, h:h + 1], scale=SLOPE).then_inc(ev["rows"], 1)

            def sums(*widths):
                v = k.event("sums") - 1
                if not (isinstance(v, int) and v <= 0):
                    act.wait_ge(s_attf, v)
                o = 0
                for b, w in enumerate(widths):
                    got(b)
                    af(att[:, o:o + w], bank[b][:, 0:w], ACT.Copy).then_inc(ev["att"], 1)
                    o += w

            def y_slot(slots):
                v = k.event("y") - slots
                if not (isinstance(v, int) and v <= 0):
                    act.wait_ge(s_acc, v)

            def scores():
                ln_out()
                got(4)
                af(sc[:, :, :], bank[4][:, 0:CT * E0].rearrange("p (t e) -> p t e", e=E0),
                   ACT.Copy).then_inc(ev["sc"], 1)

            def gate():
                act.wait_ge(s_gap, k.event("gap"))
                af(gst[:, 3, :], gst[:, 2, :], ACT.Exp).then_inc(s_gex, 1)

            def combine():
                got(6)
                af(combT[:, :, :], bank[6][0:E0, :].rearrange("p (t i) -> p t i", i=P),
                   ACT.Copy).then_inc(ev["combT"], 1)
                y_slot(3)
                got(5)
                af(ysb[:, 2, :], bank[5][:, :], ACT.Copy).then_inc(ev["y"], 1)

            def first_layer(pair):
                for e in (2 * pair, 2 * pair + 1):
                    for c in range(HC):
                        got(HB[c])
                        af(hid[:, e % 2, c, :], bank[HB[c]][:, :], ACT.Relu,
                           bias=b1[:, e, c:c + 1]).then_inc(ev["hid"], 1)

            def second_layer(e):
                if e == 0:
                    act.wait_ge(s_comb, k.event("comb"))
                y_slot(3)
                got(4 + e % 2)
                for i in range(CT):
                    last = af(ysb[:, (e if e < 2 else e + 1) % 3, i * P:(i + 1) * P],
                              bank[4 + e % 2][:, i * P:(i + 1) * P], ACT.Copy, scale=comb[:, i, e:e + 1])
                last.then_inc(ev["y"], 1)

            for r in range(CT):
                mask_rows(r)
            got(6)
            af(wxs[0][:, P:XC], bank[6][:, 0:8], ACT.Copy)
            af(wxs[1][:, P:XC], bank[6][:, 8:16], ACT.Copy)
            af(bac[:, :], bank[6][:, 16:24], ACT.Copy).then_inc(ev["ext"], 1)
            for c in range(C):
                ln_out(c, (6, 4)[c % 2])
                project(whx0, c)
            for h in range(H):
                source_row(h)
            got(6)
            af(wnorm[:, :], bank[6][:, 0:2 * H + 1], ACT.Copy).then_inc(ev["bound"], 1)
            act.wait_ge(s_arg, 1)
            af(bd[:, :, :, 0], dsh[:, :, :], ACT.Exp, bias=consts[:, 0:1])
            af(bd[:, :, :, 1], dsh[:, :, :], ACT.Exp, bias=consts[:, 1:2], scale=SLOPE).then_inc(s_exp, 1)
            act.wait_ge(s_arg, 2)
            af(ab[:, :, :, 0], arg[:, :, :, 0], ACT.Exp, bias=consts[:, 2:3])
            af(ab[:, :, :, 1], arg[:, :, :, 1], ACT.Exp, bias=consts[:, 3:4]).then_inc(s_exp, 1)

            def above(n, h, q):
                if isinstance(n, int) and n == 0:
                    pass
                elif q < Q - 1:
                    act.wait_ge(s_indf, n * (Q - 1) + (q + 1 - (Q - 1)))
                else:
                    act.wait_ge(full[1], n)
                for j in range(QT):
                    last = af(ind[:, q, 1, j, :], sbc[:, h, :], ACT.Relu, bias=nd[:, q * QT + j, h:h + 1],
                              scale=BIG)
                last.then_inc(s_above, 1)

            def head(c, h):
                above(c * H + h + 1, (h + 1) % H, 1)
                sums(4 * VW, 4 * VW)
                source_row(h)

            for q in range(1, Q):
                above(0, 0, q)
                if q < 3:
                    mask_rows(CT + q - 1)
            act.wait_ge(s_xb, C)
            for h in range(H):
                head(0, h)
                if h == 2:
                    act.wait_ge(s_u, H)
                rows = list(ROWS[h])
                for q in (2, 3):
                    for r in rows[q - 2:q - 1]:
                        mask_rows(r)
                    above(h + 1, (h + 1) % H, q)
                for r in rows[2:]:
                    mask_rows(r)
            per = {"sums": 4, "full0": 4, "full1": 4, "full6": 12, "full7": 10, "full4": 5, "gap": 1, "comb": 1,
                   "full5": 5, "y": 9, "full2": 8, "full3": 8}
            act.wait_ge(s_w2, 16 * NW2)

            def chunk0(c):
                scores()
                first_layer(0)
                gate()
                for h in range(H):
                    head(c, h)
                    if h:
                        first_layer(h)
                    for e in (2 * h, 2 * h + 1):
                        above(c * H + h + 1, (h + 1) % H, 2 + e % 2)
                        second_layer(e)
                    if h == 0:
                        combine()

            chunk0(1)
            with act.Fori(2, C) as c:
                k.enter(c, 2, per)
                chunk0(c)
                k.leave(C - 2, per)
            def prepare1(c):
                tiles = slice(c * CT, (c + 1) * CT)
                ln_out(c)
                project(whx1, c)
                act.wait_ge(ev["proj"], 2 * C + 2 * (c + 1))
                act.wait_ge(s_nmx, 1)
                for h in range(H):
                    af(nd[:, tiles, h], whx1[:, tiles, P + H + h], ACT.Exp, bias=nmx[:, h:h + 1], scale=-SLOPE)
                af(v1[:, tiles, P], whx1[:, tiles, XC], ACT.Exp, bias=nmx[:, H:H + 1]).then_inc(s_exp, 1)
                if c < 2:
                    source_rows1(c)

            scores()
            for h in range(H):
                first_layer(h)
                if h == 0:
                    gate()
                elif h < 3:
                    prepare1(h)
                for e in (2 * h, 2 * h + 1):
                    second_layer(e)
                if h == 0:
                    combine()
                    prepare1(0)
            prepare1(3)
            sums(3 * (P + 1), P + 1)

            def hidden(i):
                b = 2 + i % 2 * 2
                got(b)
                for m in range(KC):
                    last = af(htt[:, i % 2, 0, m * P:(m + 1) * P], bank[b][:, m * P:(m + 1) * P], ACT.Relu,
                              bias=bi[:, m:m + 1])
                last.then_inc(ev["htt"], 1)

            def layer(i):
                b = 3 + i % 2 * 2
                got(b)
                af(hn[:, i % 2, :], bank[b][:, 0:HID], ACT.Relu).then_inc(ev["htt"], 1)

            def turn(i, l):
                b = 2 + i % 2 * 2
                got(b)
                af(htt[:, i % 2, l + 1, :], bank[b][:, 0:HID], ACT.Copy).then_inc(ev["htt"], 1)

            def output(i):
                b = 3 + i % 2 * 2
                y_slot(CT)
                got(b)
                af(ysb[:, 0, i * P:(i + 1) * P], bank[b][:, 0:P], ACT.Copy).then_inc(ev["y"], 1)

            per = {"sums": 1, "full0": 1, "full1": 1, "full6": 3, "full7": 2, "full2": 6, "full3": 6,
                   "full4": 6, "full5": 6, "y": 4}
            with act.Fori(1, C) as c:
                k.enter(c, 1, per)
                ln_out()
                hidden(0)
                for i in range(CT):
                    layer(i)
                    if i == 0:
                        source_rows1((c + 1) % 2)
                    turn(i, 0)
                    layer(i)
                    if i == CT - 1:
                        sums(3 * (P + 1), P + 1)
                    turn(i, 1)
                    if i < CT - 1:
                        hidden(i + 1)
                    output(i)
                k.leave(C - 1, per)
            ln_out()
            for i in range(0, CT, 2):
                pair = (i, i + 1)
                for j in pair:
                    hidden(j)
                for l in range(L):
                    for j in pair:
                        layer(j)
                    for j in pair:
                        turn(j, l)
                for j in pair:
                    output(j)

        @block.vector
        def _(dve):
            k = Count()
            v = nc.vector

            def then(ins):
                ins.then_inc(s_dve, 1)
                dve.wait_ge(s_dve, k.event("dve"))

            def statistics(t0, at=0):
                for i in range(CT):
                    last = v.bn_stats(out=halves[:, at + i, :], in_=x[:, t0 + i, :])
                return last

            def moments_of(n):
                mean = [halves[:, 0:n, 1], halves[:, 0:n, 4]]
                v.tensor_tensor(step[:, 0:n], mean[0], mean[1], ALU.subtract)
                v.tensor_tensor(means[:, 0:n], mean[0], mean[1], ALU.add)
                then(v.tensor_tensor(var[:, 0:n], halves[:, 0:n, 2], halves[:, 0:n, 5], ALU.add))
                v.tensor_scalar(means[:, 0:n], means[:, 0:n], 0.5, None, ALU.mult)
                then(v.tensor_tensor(step[:, 0:n], step[:, 0:n], step[:, 0:n], ALU.mult))
                then(v.scalar_tensor_tensor(var[:, 0:n], step[:, 0:n], P / 4.0, var[:, 0:n], ALU.mult, ALU.add))

            def deviations(n):
                moments_of(n)
                then(v.tensor_scalar(var[:, 0:n], var[:, 0:n], 1.0 / P, EPS, ALU.mult, ALU.add))
                inverse_root(n)

            def scale(t0, to=xn, at=0):
                for i in range(CT):
                    last = v.tensor_scalar(to[:, i, :], x[:, t0 + i, :], means[:, at + i:at + i + 1],
                                           rstd[:, at + i:at + i + 1], ALU.subtract, ALU.mult)
                last.then_inc(s_xn, 1)

            def inverse_root(n):
                v.tensor_scalar(nhalf[:, 0:n], var[:, 0:n], -0.5, None, ALU.mult)
                then(v.tensor_scalar(rstd[:, 0:n].bitcast(I32), var[:, 0:n].bitcast(I32), -0.5, 1597463007.0,
                                     ALU.mult, ALU.add))
                for _ in range(3):
                    then(v.tensor_tensor(step[:, 0:n], rstd[:, 0:n], rstd[:, 0:n], ALU.mult))
                    then(v.tensor_tensor(step[:, 0:n], step[:, 0:n], nhalf[:, 0:n], ALU.mult))
                    then(v.scalar_tensor_tensor(rstd[:, 0:n], step[:, 0:n], 1.5, rstd[:, 0:n], ALU.add, ALU.mult))

            def norm(c, unit):
                dve.wait_ge(ev["hTc"], unit)
                if not isinstance(c, int):
                    v.memset(waited[:, :], 0.0)
                then(statistics(c * CT))
                deviations(CT)
                scale(c * CT)

            for c in range(C):
                dve.wait_ge(s_x[c], 16)
                last = statistics(c * CT, c * CT)
            then(last)
            deviations(T)
            for c in range(C):
                if c >= 2:
                    dve.wait_ge(ev["hTc"], c - 1)
                scale(c * CT, (xn, odiv)[c % 2], c * CT)
                if c == 0:
                    dve.wait_ge(s_const, NC)
                    dve.wait_ge(s_w, 16 * NW)
                    v.tensor_scalar(brep, ones[:, :], bcol[:, 0:1], None, ALU.mult).then_inc(s_brep, 1)
            dve.wait_ge(ev["ext"], 1)

            def replicate(s):
                for h in range(H):
                    v.tensor_scalar(wrep[:, h, :], ones[:, :], wxs[s][:, P + h:P + h + 1], None,
                                    ALU.mult).then_inc(s_rep, 1)

            replicate(0)
            wm = wxs[1][:, XC:XM]
            then(v.reduce_sum(wm, wxs[1][:, P + H:XC], AX_X))
            then(v.tensor_scalar(wm, wm, 1.0 / H, None, ALU.mult))
            v.tensor_tensor(wsq[:, :], wxs[1][:, P:XM], wxs[1][:, P:XM], ALU.mult).then_inc(s_wsq, 1)
            then(v.tensor_tensor(bsum[:, :], bac[:, 0:H], bac[:, H:2 * H], ALU.add))

            def indicate(c, h, quads=range(Q)):
                n = c * H + h
                cs = bass.ts(c, CW)
                for q in quads:
                    if q:
                        dve.wait_ge(s_above, n * (Q - 1) + q)
                        last = v.tensor_tensor(ind[:, q, 0, :, :], maskT[:, q * QT:(q + 1) * QT, cs],
                                               ind[:, q, 1, :, :], ALU.min)
                    else:
                        dve.wait_ge(ev["rows"], n + 1)
                        if not (isinstance(n, int) and n == 0):
                            dve.wait_ge(s_indf, (n - 1) * (Q - 1) + 1)
                        for t in range(QT):
                            last = v.scalar_tensor_tensor(ind[:, 0, 0, t, :], sbc[:, h, :], thr[:, t, h:h + 1],
                                                          maskT[:, t, cs], ALU.is_gt, ALU.mult)
                    last.then_inc(s_g, 1)
                    dve.wait_ge(s_g, n * Q + (q + 1))
                    v.tensor_tensor(ind[:, q, 1, :, :], maskT[:, q * QT:(q + 1) * QT, cs], ind[:, q, 0, :, :],
                                    ALU.subtract).then_inc(s_ind, 1)

            dve.wait_ge(ev["proj"], 2 * C)
            S0, D0 = whx0[:, :, P:P + H], whx0[:, :, P + H:P + 2 * H]
            then(v.tensor_tensor(nd[:, :, :], D0, bsum[:, :].unsqueeze(1).to_broadcast([P, T, H]), ALU.add))
            then(v.tensor_scalar(thr[:, :, :], nd[:, 0:QT, :], -1.0, None, ALU.mult))
            then(v.tensor_scalar(nd[:, :, :], nd[:, :, :], BIG, None, ALU.mult))
            v.tensor_reduce(pmax[:, :], D0.rearrange("p t h -> p h t"), AX_X, ALU.max).then_inc(s_pm, 1)
            dve.wait_ge(s_gm, 1)
            g0 = gmax[:, :].unsqueeze(1).to_broadcast([P, T, H])
            v.tensor_tensor(dsh[:, :, :], D0, g0, ALU.subtract).then_inc(s_arg, 1)
            then(v.tensor_tensor(gb[:, :], gmax[:, :], bsum[:, :], ALU.add))
            then(v.tensor_tensor(zt[:, :, :], S0, gb[:, :].unsqueeze(1).to_broadcast([P, T, H]), ALU.add))
            then(v.scalar_tensor_tensor(zm[:, :, :], zt[:, :, :], SLOPE, zt[:, :, :], ALU.mult, ALU.max))
            v.tensor_tensor(arg[:, :, :, 0], zt[:, :, :], zm[:, :, :], ALU.subtract)
            v.scalar_tensor_tensor(arg[:, :, :, 1], zt[:, :, :], SLOPE, zm[:, :, :], ALU.mult,
                                   ALU.subtract).then_inc(s_arg, 1)
            dve.wait_ge(ev["mask"], 2 * CT)
            indicate(0, 0, range(1))
            dve.wait_ge(s_exp, 1)
            split(v, 0, then)

            def merge(c, h):
                n = c * H + h
                dve.wait_ge(ev["att"], n * 2 + 2)
                a4 = att[:, :].rearrange("p (g s v) -> p g s v", s=PARTS, v=V1)
                then(v.tensor_tensor(red[:, :, :], a4[:, :, 1, :], a4[:, :, 2, :], ALU.add))
                v.tensor_tensor(red[:, :, :], red[:, :, :], a4[:, :, 0, :], ALU.add).then_inc(s_attf, 1)
                dve.wait_ge(s_attf, n + 1)
                dve.wait_ge(s_exp, 2)
                then(v.tensor_tensor(wred[:, :, :].rearrange("p (t b) v -> p t b v", b=2),
                                     red[:, :, :].rearrange("p (t b) v -> p t b v", b=2),
                                     more(ab[:, bass.ts(c, CT), h, :], V1), ALU.mult))
                w4 = wred[:, :, :].rearrange("p (t b) v -> p t b v", b=2)
                then(v.tensor_tensor(num[:, :, :], w4[:, :, 0, :], w4[:, :, 1, :], ALU.add))
                then(v.reciprocal(rden[:, :], num[:, :, DH]))
                then(v.tensor_tensor(odiv[:, :, 0:DH], num[:, :, 0:DH], more(rden[:, :], DH), ALU.mult))
                xo = x[:, bass.ts(c, CT), h * DH:(h + 1) * DH]
                then(v.tensor_tensor(xo, xo, odiv[:, :, 0:DH], ALU.add))

            def best(c, unit):
                dve.wait_ge(ev["sc"], unit - C + 1)
                fw = first_w[:, :].unsqueeze(1).to_broadcast([P, CT, E0])
                src = sc
                for r in range(2):
                    then(v.tensor_reduce(gst[:, r, :], src[:, :, :], AX_X, ALU.max))
                    then(v.tensor_tensor(key[:, :, :], src[:, :, :], more(gst[:, r, :], E0), ALU.is_equal))
                    then(v.tensor_tensor(key[:, :, :], key[:, :, :], fw, ALU.mult))
                    then(v.tensor_reduce(gst[:, 4, :], key[:, :, :], AX_X, ALU.max))
                    then(v.tensor_tensor(oh[:, r, :, :], key[:, :, :], more(gst[:, 4, :], E0), ALU.is_equal))
                    if r == 0:
                        then(v.scalar_tensor_tensor(sc2[:, :, :], oh[:, 0, :, :], NEG, sc[:, :, :], ALU.mult,
                                                    ALU.add))
                        src = sc2
                v.tensor_tensor(gst[:, 2, :], gst[:, 1, :], gst[:, 0, :], ALU.subtract).then_inc(s_gap, 1)

            def gate(c, unit):
                dve.wait_ge(s_gex, unit - C + 1)
                then(v.tensor_scalar(gst[:, 5, :], gst[:, 3, :], 1.0, None, ALU.add))
                then(v.reciprocal(gst[:, 6, :], gst[:, 5, :]))
                then(v.tensor_tensor(gst[:, 7, :], gst[:, 3, :], gst[:, 6, :], ALU.mult))
                v.tensor_tensor(key[:, :, :], oh[:, 1, :, :], more(gst[:, 7, :], E0), ALU.mult)
                then(v.tensor_tensor(sc2[:, :, :], oh[:, 0, :, :], more(gst[:, 6, :], E0), ALU.mult))
                v.tensor_tensor(comb[:, :, :], key[:, :, :], sc2[:, :, :], ALU.add).then_inc(s_comb, 1)

            for h in range(H):
                indicate(0, h, range(0 if h else 1, Q))
                if h == 1:
                    dve.wait_ge(s_xb, C)
                if h:
                    merge(0, h - 1)
            per = {"dve": 4 * 6 + 15 + 15}
            with dve.Fori(1, C) as c:
                k.enter(c, 1, per)
                merge(c - 1, H - 1)
                norm(c - 1, c - 1 + C)
                dve.wait_ge(ev["mask"], c * 2 * CT + 2 * CT)
                indicate(c, 0, range(2))
                best(c - 1, c - 1 + C)
                indicate(c, 0, range(2, Q))
                gate(c - 1, c - 1 + C)
                for h in range(1, H):
                    indicate(c, h)
                    merge(c, h - 1)
                k.leave(C - 1, per)
            merge(C - 1, H - 1)
            norm(C - 1, 2 * C - 1)
            best(C - 1, 2 * C - 1)
            gate(C - 1, 2 * C - 1)

            then(v.tensor_tensor(wnorm[:, 0:H], wnorm[:, 0:H], wnorm[:, H:2 * H], ALU.max))
            v.tensor_scalar(var[:, 0:H], wnorm[:, 0:H], float(P), None, ALU.mult)
            then(v.tensor_scalar(var[:, H:H + 1], wnorm[:, 2 * H:2 * H + 1], float(P), None, ALU.mult))
            inverse_root(H + 1)
            then(v.tensor_tensor(var[:, 0:H + 1], var[:, 0:H + 1], rstd[:, 0:H + 1], ALU.mult))
            v.tensor_scalar(nmx[:, 0:H], var[:, 0:H], -SLOPE, LIFT, ALU.mult, ALU.add)
            v.tensor_scalar(nmx[:, H:H + 1], var[:, H:H + 1], -1.0, None, ALU.mult).then_inc(s_nmx, 1)
            replicate(1)

            def norm1(c):
                dve.wait_ge(s_acc, (c + 1) * (E0 + 1))
                dve.wait_ge(ev["hTc"], 2 * C + c)
                then(statistics(c * CT))
                deviations(CT)
                scale(c * CT)

            def probabilities(c, first, quads, prob=prob, ready=s_prob):
                cs = bass.ts(c, CW)
                for q in quads:
                    if q >= 2:
                        dve.wait_ge(s_probf, c * (Q - 1) + (q - 1))
                    elif not first:
                        if q == 0:
                            dve.wait_ge(s_probf, c * (Q - 1))
                        else:
                            dve.wait_ge(full[1], c + C * H)
                    for h in range(H):
                        before = k.at("step") - QT
                        for j in range(QT):
                            t = q * QT + j
                            if h:
                                dve.wait_ge(s_step, before + j + 1)
                            last = v.scalar_tensor_tensor(
                                prob[:, t % 8, :], rows1[:, bass.ds((c % 2 * H + h) * CW, CW)], nd[:, t, h:h + 1],
                                maskT[:, t, cs] if h == 0 else prob[:, t % 8, :], ALU.max, ALU.mult)
                            last.then_inc(s_step if h < H - 1 else ready, 1)
                        if h < H - 1:
                            k.event("step", QT)

            def merge1(c):
                dve.wait_ge(ev["att"], c * 2 + (2 * C * H + 2))
                a3 = att[:, 0:CT * (P + 1)].rearrange("p (t v) -> p t v", v=P + 1)
                then(v.reciprocal(rden[:, :], a3[:, :, P]))
                for i in range(CT):
                    xo = x[:, c * CT + i, :]
                    last = v.scalar_tensor_tensor(xo, a3[:, i, 0:P], rden[:, i:i + 1], xo, ALU.mult, ALU.add)
                last.then_inc(s_attf, 1)
                dve.wait_ge(s_attf, c + (C * H + 1))

            norm1(0)
            norm1(1)
            for q in range(Q):
                if q == 0:
                    dve.wait_ge(ev["rows"], H * (C + 2))
                if q == Q - 1:
                    dve.wait_ge(ev["rows"], H * (C + 3))
                    probabilities(1, True, range(1))
                dve.wait_ge(s_exp, 3 + q)
                probabilities(0, True, range(q, q + 1), prob0, s_prob0)
                if q in (0, 2):
                    norm1(2 + q // 2)
            per = {"dve": 1 + 15, "step": T * (H - 1)}

            def rest(c):
                merge1(c - 1)
                norm(c - 1, c - 1 + 3 * C)
                probabilities(c, False, range(1, Q))

            with dve.Fori(1, C - 1) as c:
                k.enter(c, 1, per)
                rest(c)
                dve.wait_ge(ev["rows"], c * H + H * (C + 3))
                probabilities(c + 1, False, range(1))
                k.leave(C - 2, per)
            rest(C - 1)
            merge1(C - 1)
            norm(C - 1, 4 * C - 1)


def kernel(**inputs):
    import concourse.bacc as bacc
    from concourse.bass_utils import run_bass_kernel_spmd

    w = {n: np.asarray(v) for n, v in inputs.items()}
    lay = {
        "x": w["x"], "adj": w["adj"],
        "gW0": w["L0_gnn_W"], "gWT0": w["L0_gnn_W"].T, "gb0": w["L0_gnn_b"].reshape(1, P), "ga0": w["L0_gnn_a"],
        "gW1": w["L1_gnn_W"], "gWT1": w["L1_gnn_W"].T, "ga1": w["L1_gnn_a"].reshape(1, 2 * DH),
        "wgT": w["L0_ffn_Wg"].T, "bg": w["L0_ffn_bg"].reshape(1, E0),
        "w1T": w["L0_ffn_W1"].transpose(2, 0, 1),
        "b1": w["L0_ffn_b1"].reshape(E0, HC, P).transpose(2, 0, 1),
        "w2T": w["L0_ffn_W2"].reshape(E0, P, HC, P).transpose(3, 0, 2, 1), "b2": w["L0_ffn_b2"],
        "route": w["L1_ffn_route_id"].reshape(1, N // GRP),
        "wiT": w["L1_ffn_Wi"].T, "bi": w["L1_ffn_bi"].reshape(KC, P).T,
        "wrT": w["L1_ffn_Wr"].reshape(L, E1, HID, KC, P).transpose(4, 0, 1, 3, 2).reshape(P, L, E1, KC * HID),
        "br": w["L1_ffn_br"].transpose(1, 0, 2),
        "wsT": w["L1_ffn_Ws"].reshape(L, HID, KC, P).transpose(3, 0, 2, 1).reshape(P, L, KC * HID),
        "bs": w["L1_ffn_bs"].reshape(1, L, HID),
        "woT": w["L1_ffn_Wo"].reshape(P, KC, P).transpose(2, 1, 0), "bo": w["L1_ffn_bo"].reshape(1, P),
    }
    nc = bacc.Bacc("TRN2", target_bir_lowering=False, num_devices=1)
    arrays, args = {}, {}
    for name, v in lay.items():
        v = np.ascontiguousarray(v)
        arrays[f"in_{name}"] = v
        args[name] = nc.dram_tensor(f"in_{name}", v.shape, mybir.dt.from_np(v.dtype), kind="ExternalInput").ap()
    out = nc.dram_tensor("out_x", (N, P), F32, kind="ExternalOutput").ap()
    gnn_moe_stack(nc, args, out)
    r = run_bass_kernel_spmd(nc, [arrays], core_ids=[0])
    return r.results[0]["out_x"]
```
